# Optimizing a Trainium2 kernel written in Bass

```python
import numpy as np
import jax
import jax.numpy as jnp

def _softmax(x, axis=-1):
    return jax.nn.softmax(x, axis=axis)

def _gelu(x):
    return jax.nn.gelu(x, approximate=True)

def _silu(x):
    return jax.nn.silu(x)

def _sigmoid(x):
    return jax.nn.sigmoid(x)

def _layernorm(x, axis=-1, eps=1e-05):
    m = jnp.mean(x, axis=axis, keepdims=True)
    v = jnp.var(x, axis=axis, keepdims=True)
    return (x - m) / jnp.sqrt(v + eps)

def _scatter_add(tgt, idx, src, axis=0):
    return tgt.at[idx].add(src)

def _segment_sum(src, seg, n):
    return jax.ops.segment_sum(src, seg, n)
kernel_name = 'mk_adj_preln_d4_adj_r2_c31503'

def setup_inputs(seed: int=0):
    np.random.seed(seed)
    _w = jnp.asarray

    def _rec_inputs():
        import jax
        import jax.numpy as jnp
        _gk = jax.random.key(seed)
        x = -0.000929 + 1 * jax.random.normal(jax.random.fold_in(_gk, 1), (4096, 128), jnp.float32)
        _a = jax.random.bernoulli(jax.random.fold_in(_gk, 2), 0.00195312, (4096, 4096))
        _a = jnp.logical_or(_a, jnp.swapaxes(_a, -1, -2))
        _a = jnp.logical_or(_a, jnp.eye(4096, dtype=bool))
        _af = _a.astype(jnp.float32)
        adj = _af
        return (x, adj)
    x, adj = _rec_inputs()

    def _L0_gnn_setup():
        import jax, jax.numpy as jnp
        import numpy as np
        N, D = (4096, 128)
        EDGE_PROB = 0.005
        COS_EPS = 1e-08
        key = jax.random.key(seed)
        kx, ka = jax.random.split(key)
        x = jax.random.normal(kx, (N, D), dtype=jnp.float32)
        adj = (jax.random.uniform(ka, (N, N)) < EDGE_PROB).astype(jnp.float32)
        return {'t': jnp.float32(0.0), 'x': x, 'adj': adj, 'alpha': jnp.float32(0.5), 'beta': jnp.float32(1.0)}
    _L0_gnn_all = _L0_gnn_setup()
    _L0_gnn_in = {k: v for k, v in _L0_gnn_all.items() if k in ('t', 'alpha', 'beta')}
    del _L0_gnn_all

    def _L1_gnn_setup():
        import jax, jax.numpy as jnp
        import numpy as np
        N = 4096
        F_IN = 128
        F_OUT = 128
        key = jax.random.key(seed)
        k1, k2, k3, k4, k5 = jax.random.split(key, 5)
        x = jax.random.normal(k1, (N, F_IN), dtype=jnp.float32)
        adj = jax.random.uniform(k2, (N, N), dtype=jnp.float32)
        kernel = jax.random.normal(k3, (F_IN, F_OUT), dtype=jnp.float32) * 0.05
        bias = jax.random.normal(k4, (F_OUT,), dtype=jnp.float32) * 0.05
        beta = jax.random.uniform(k5, (N,), dtype=jnp.float32)
        return {'x': x, 'adj': adj, 'kernel': kernel, 'bias': bias, 'beta': beta}
    _L1_gnn_all = _L1_gnn_setup()
    _L1_gnn_in = {k: v for k, v in _L1_gnn_all.items() if k in ('kernel', 'bias', 'beta')}
    del _L1_gnn_all

    def _L2_gnn_setup():
        import jax, jax.numpy as jnp
        import numpy as np
        N = 8192
        C = 128
        F = 128
        key = jax.random.key(seed)
        k1, k2, k3, k4 = jax.random.split(key, 4)
        X = jax.random.normal(k1, (N, C), dtype=jnp.float32)
        adj = jax.random.uniform(k2, (N, N), dtype=jnp.float32)
        W = jax.random.normal(k3, (C, F), dtype=jnp.float32) * 0.05
        b = jax.random.normal(k4, (F,), dtype=jnp.float32) * 0.05
        return {'X': X, 'adj': adj, 'W': W, 'b': b}
    _L2_gnn_all = _L2_gnn_setup()
    _L2_gnn_in = {k: v for k, v in _L2_gnn_all.items() if k in ('W', 'b')}
    del _L2_gnn_all

    def _L3_gnn_setup():
        import jax, jax.numpy as jnp
        import numpy as np
        EPS = 1e-07
        MAX_TANH = 1.0 - 1e-06

        def _norm(v):
            return jnp.maximum(jnp.linalg.norm(v, axis=-1, keepdims=True), EPS)

        def log_map_zero(y):
            n = _norm(y)
            return jnp.arctanh(jnp.clip(n, 0.0, MAX_TANH)) * y / n

        def exp_map_zero(v):
            n = _norm(v)
            return jnp.tanh(n) * v / n

        def h_add(x, y):
            xy = jnp.sum(x * y, axis=-1, keepdims=True)
            x2 = jnp.sum(x * x, axis=-1, keepdims=True)
            y2 = jnp.sum(y * y, axis=-1, keepdims=True)
            num = (1.0 + 2.0 * xy + y2) * x + (1.0 - x2) * y
            den = 1.0 + 2.0 * xy + x2 * y2
            return num / jnp.maximum(den, EPS)

        def h_mul(x, W):
            return exp_map_zero(log_map_zero(x) @ W)
        key = jax.random.key(seed)
        k1, k2, k3, k4 = jax.random.split(key, 4)
        N, F_IN, F_OUT = (4096, 128, 128)
        x = 0.05 * jax.random.normal(k1, (N, F_IN), dtype=jnp.float32)
        a = (jax.random.uniform(k2, (N, N)) < 0.01).astype(jnp.float32)
        adj = a / jnp.maximum(a.sum(axis=1, keepdims=True), 1.0)
        lim_e = np.sqrt(6.0 / (F_IN + F_IN)) * np.sqrt(2.0)
        lim_l = np.sqrt(6.0 / (2 * F_IN + F_OUT)) * np.sqrt(2.0)
        embed = jax.random.uniform(k3, (F_IN, F_IN), minval=-lim_e, maxval=lim_e, dtype=jnp.float32)
        layer = jax.random.uniform(k4, (2 * F_IN, F_OUT), minval=-lim_l, maxval=lim_l, dtype=jnp.float32)
        embed_bias = jnp.zeros((F_IN,), dtype=jnp.float32)
        layer_bias = jnp.zeros((F_OUT,), dtype=jnp.float32)
        return {'x': x, 'adj': adj, 'embed': embed, 'layer': layer, 'embed_bias': embed_bias, 'layer_bias': layer_bias}
    _L3_gnn_all = _L3_gnn_setup()
    _L3_gnn_in = {k: v for k, v in _L3_gnn_all.items() if k in ('embed', 'layer', 'embed_bias', 'layer_bias')}
    del _L3_gnn_all
    return {'x': x, 'adj': adj, 'L0_gnn_t': _L0_gnn_in['t'], 'L0_gnn_alpha': _L0_gnn_in['alpha'], 'L0_gnn_beta': _L0_gnn_in['beta'], 'L1_gnn_kernel': _L1_gnn_in['kernel'], 'L1_gnn_bias': _L1_gnn_in['bias'], 'L1_gnn_beta': _L1_gnn_in['beta'], 'L2_gnn_W': _L2_gnn_in['W'], 'L2_gnn_b': _L2_gnn_in['b'], 'L3_gnn_embed': _L3_gnn_in['embed'], 'L3_gnn_layer': _L3_gnn_in['layer'], 'L3_gnn_embed_bias': _L3_gnn_in['embed_bias'], 'L3_gnn_layer_bias': _L3_gnn_in['layer_bias']}

def reference(x, adj, L0_gnn_t, L0_gnn_alpha, L0_gnn_beta, L1_gnn_kernel, L1_gnn_bias, L1_gnn_beta, L2_gnn_W, L2_gnn_b, L3_gnn_embed, L3_gnn_layer, L3_gnn_embed_bias, L3_gnn_layer_bias):
    import jax
    import jax.numpy as jnp

    def _L0_gnn_ref(t, x, adj, alpha, beta):
        import jax, jax.numpy as jnp
        import numpy as np
        N, D = (4096, 128)
        EDGE_PROB = 0.005
        COS_EPS = 1e-08
        deg = jnp.clip(adj.sum(axis=1), 1.0)
        dis = deg ** (-0.5)
        adj_norm = dis[:, None] * adj * dis[None, :]
        diffusion = adj_norm @ x - x
        norms = jnp.maximum(jnp.linalg.norm(x, axis=-1), COS_EPS)
        sim = x @ x.T / (norms[:, None] * norms[None, :])
        attn = jax.nn.softmax(beta * sim * adj, axis=1)
        attn = jax.lax.stop_gradient(attn)
        return diffusion + jax.nn.sigmoid(alpha) * (attn @ x - x)

    def _L1_gnn_ref(x, adj, kernel, bias, beta):
        import jax, jax.numpy as jnp
        import numpy as np
        N = 4096
        F_IN = 128
        F_OUT = 128
        inv_deg = 1.0 / (jnp.sum(adj, axis=1) + beta)
        agg = adj @ x + beta[:, None] * x
        out = inv_deg[:, None] * agg @ kernel + bias
        return out

    def _L2_gnn_ref(X, adj, W, b):
        import jax, jax.numpy as jnp
        import numpy as np
        N = 8192
        C = 128
        F = 128
        adj_hat = adj + jnp.eye(adj.shape[0], dtype=adj.dtype)
        d_inv_sqrt = 1.0 / jnp.sqrt(jnp.sum(adj_hat, axis=1))
        adj_norm = adj_hat * d_inv_sqrt[:, None] * d_inv_sqrt[None, :]
        out = adj_norm @ (X @ W) + b
        return jax.nn.relu(out)

    def _L3_gnn_ref(x, adj, embed, layer, embed_bias, layer_bias):
        import jax, jax.numpy as jnp
        import numpy as np
        EPS = 1e-07
        MAX_TANH = 1.0 - 1e-06

        def _norm(v):
            return jnp.maximum(jnp.linalg.norm(v, axis=-1, keepdims=True), EPS)

        def log_map_zero(y):
            n = _norm(y)
            return jnp.arctanh(jnp.clip(n, 0.0, MAX_TANH)) * y / n

        def exp_map_zero(v):
            n = _norm(v)
            return jnp.tanh(n) * v / n

        def h_add(x, y):
            xy = jnp.sum(x * y, axis=-1, keepdims=True)
            x2 = jnp.sum(x * x, axis=-1, keepdims=True)
            y2 = jnp.sum(y * y, axis=-1, keepdims=True)
            num = (1.0 + 2.0 * xy + y2) * x + (1.0 - x2) * y
            den = 1.0 + 2.0 * xy + x2 * y2
            return num / jnp.maximum(den, EPS)

        def h_mul(x, W):
            return exp_map_zero(log_map_zero(x) @ W)
        h = h_mul(x, embed)
        h = h_add(h, embed_bias[None, :])
        neigh = exp_map_zero(adj @ log_map_zero(h))
        out = h_mul(jnp.concatenate((x, neigh), axis=1), layer)
        out = h_add(out, layer_bias[None, :])
        return out
    h = jnp.maximum(_layernorm(x, axis=-1), 0.0)
    x = x + _L0_gnn_ref(L0_gnn_t, h, adj, L0_gnn_alpha, L0_gnn_beta)
    h = jnp.maximum(_layernorm(x, axis=-1), 0.0)
    x = x + _L1_gnn_ref(h, adj, L1_gnn_kernel, L1_gnn_bias, L1_gnn_beta)
    h = jnp.maximum(_layernorm(x, axis=-1), 0.0)
    x = x + _L2_gnn_ref(h, adj, L2_gnn_W, L2_gnn_b)
    h = jnp.maximum(_layernorm(x, axis=-1), 0.0)
    x = x + _L3_gnn_ref(h, adj, L3_gnn_embed, L3_gnn_layer, L3_gnn_embed_bias, L3_gnn_layer_bias)
    return x

_drawn_inputs = setup_inputs


def setup_inputs(seed=0):
    import zlib

    import numpy as np

    out = dict(_drawn_inputs(seed))
    spreads = {'L3_gnn_embed_bias': (0.0, 0.8), 'L3_gnn_layer_bias': (0.0, 0.8)}
    factors = {'L1_gnn_beta': 8.0, 'L3_gnn_embed': 3.164}
    for name, (base, spread) in spreads.items():
        noise = np.random.default_rng([zlib.crc32(name.encode()), seed]).standard_normal(out[name].shape)
        drawn = base * np.exp(spread * noise) if base else spread * noise
        out[name] = jnp.asarray(drawn.astype(out[name].dtype))
    for name, factor in factors.items():
        out[name] = (out[name] * factor).astype(out[name].dtype)
    return out
```

```python
from contextlib import ExitStack

import concourse.bass as bass
from concourse import mybir

F32, F16 = mybir.dt.float32, mybir.dt.float16
U8, U16, F8 = mybir.dt.uint8, mybir.dt.uint16, mybir.dt.float8e4
ALU, ACT = mybir.AluOpType, mybir.ActivationFunctionType

N, D = 4096, 128
P = 128
NB = N // P
NP = NB // 2
BC = 4
NCH = NB // BC
CW = BC * P
HALF = N // 2
HPC = 2 * BC
TPH = HALF // 2 // P
RING = 4
Z_AHEAD = 1

CAST_AT = [3 * m + r for m in range(HPC) for r in (1, 2)]
TURN_AT = [3 * m + 2 for m in range(HPC)]
PLACE_AT = [3 * m + 8 for m in range(HPC)]

H_SCALE = 4096.0
U_SCALE = 16384.0
A_BYTE = 64.0
A_VALUE = 2.0
E_SHIFT = 10.0
LN_EPS, COS_EPS, EPS = 1e-5, 1e-8, 1e-7
MAX_TANH = 1.0 - 1e-6
LINKS = (5, 4, 47, 44)
NEXT_AFTER_1 = 1.0 + 2.0 ** -23


class Chain:

    def __init__(self, eng, sem, base=0):
        self.eng, self.sem, self.base, self.n = eng, sem, base, 0

    def step(self, ins):
        self.n += 1
        self.eng.drain()


QUARTERS = ([(0, q) for q in range(7)] + [(1, q) for q in range(7)] + [(0, 7), (1, 7)]
            + [(c, q) for c in range(2, NCH) for q in range(8)])
W_AFTER = [15, 21, 27, 33, 40, 48, 56, 64]
T_AFTER = [w + 4 for w in W_AFTER]
V_AFTER = [w + 5 for w in W_AFTER]


def program(nc, x_in, adj, alpha, beta, l1_kernel, l1_bias, l1_beta, l2_w, l2_b, embed, layer,
            embed_bias, layer_bias, out):
    ctx = ExitStack()
    with ctx:
        def sb(name, shape, dt=F32):
            return ctx.enter_context(nc.sbuf_tensor(name, shape, dt))

        def sem(name):
            return ctx.enter_context(nc.semaphore(name))

        ds = bass.ds

        adj_t = sb("adj_t", [P, NP, N], U16)
        adj_u8 = adj_t[:, :, :].bitcast(U8).rearrange("p c (i t) -> p c i t", t=2)
        adj_f8 = adj_t[:, :, :].bitcast(F8).rearrange("p c (i t) -> p c i t", t=2)
        x = sb("x", [P, NB, D])
        LO, HI = 0, 1
        h_a = sb("h_a", [P, NB, 2, D + 2], F16)
        stage = sb("stage", [P, 2, HALF])
        h_c = stage[:, :, :].rearrange("p a n -> p (a n)").bitcast(F16).rearrange(
            "p (k r f) -> p k r f", r=2, f=D)
        u_t = sb("u_t", [P, 2, N], F16)
        hw = u_t[:, :, :].rearrange("p a n -> p (a n)").bitcast(F32).rearrange(
            "p (k f) -> p k f", f=D)
        bytes8 = sb("bytes8", [P, 2, HALF], U8)
        hd_f = bytes8[:, :, :].bitcast(F32)
        ez = sb("ez", [P, RING, CW])
        e_parts = sb("e_parts", [P, 2, RING, CW], F16)
        agg_sb = ez[:, 0, :]
        ht_sb = ez[:, 1, :]
        hf = ez[:, 2, :].rearrange("p (b f) -> p b f", f=D)
        g_f = ez[:, 3, :].rearrange("p (b f) -> p b f", f=D)
        ep = e_parts[:, :, :, :].rearrange("p a r n -> p (a r n)")
        hs = ep[:, 0:2 * CW].rearrange("p (b r f) -> p b r f", r=2, f=D)
        tmp = ep[:, 2 * CW:4 * CW].bitcast(F32).rearrange("p (b f) -> p b f", f=D)
        v0 = ep[:, 4 * CW:6 * CW].bitcast(F32).rearrange("p (b f) -> p b f", f=D)
        act_junk = ep[:, 6 * CW:8 * CW].bitcast(F32).rearrange("p (b f) -> p b f", f=D)
        dve_junk = bytes8[:, 0, :].bitcast(F32).rearrange("p (b f) -> p b f", f=D)
        h0f = adj_t[:, :, 4 * CW:5 * CW].bitcast(F32).rearrange("p c (t f) -> p c t f", t=2)
        u0f = adj_t[:, :, 5 * CW:6 * CW].bitcast(F32).rearrange("p c (t f) -> p c t f", t=2)
        u0p = adj_t[:, :, 6 * CW:7 * CW].bitcast(F16).rearrange("p c (t r f) -> p c t r f", r=2, t=2)

        kernel_sb = sb("kernel_sb", [D, D])
        w_sb = sb("w_sb", [D, D])
        embed_top = sb("embed_top", [D, 2, D])
        bot_ident = sb("bot_ident", [D, 2, D])
        ident32 = bot_ident[:, 1, :]
        ident16 = sb("ident16", [P, P], F16)
        ident16x2 = sb("ident16x2", [P, P], F16)
        bias_bc = sb("bias_bc", [P, 4, D])
        l1_bias_bc, l2_b_bc, eb_bc, lb_bc = (bias_bc[:, n, :] for n in range(4))
        scal = sb("scal", [P, 12])
        (alpha_c, beta_c, e_alpha, sig_c, sig_h, x_coef, beta_s, shift_c, y2_embed, y2_layer,
         neg_half, half) = (scal[:, n:n + 1] for n in range(12))
        deg_parts = sb("deg_parts", [P, NB, 4])
        cols = sb("cols", [P, 11, NB])
        (deg, dis, inv_deg, inv_beta, d2, l1b, rs0, nb0, sq_h, norm0, run0) = (
            cols[:, n, :] for n in range(11))
        st = sb("st", [P, BC, 6])
        mv = sb("mv", [P, BC, 2])
        mv0 = sb("mv0", [P, NB, 2])
        small = sb("small", [P, 26, BC])
        (rec, ve, rs, nb, n_h, l_h, v_sq, n_v, v_y, a_c, b_c, at_n, at_o, at_t, at_u, at_l, at_w,
         th_n, th_u, th_l, th_w, th, q_c, x2, a_sq, n_a) = (small[:, n, :] for n in range(26))
        small2 = sb("small2", [P, 6, BC])
        tq, cat_sq, n_cat, l_cat, h2_sq, n_h2 = (small2[:, n, :] for n in range(6))

        ps_s = ctx.enter_context(nc.psum_tensor("ps_s", [P, 4, CW], F32))
        ps_acc = ctx.enter_context(nc.psum_tensor("ps_acc", [P, 2, CW], F32))
        ps_t = ctx.enter_context(nc.psum_tensor("ps_t", [P, 2, CW], F32))
        ps_t16 = ps_t[:, :, :].bitcast(F16)
        ps_s16 = ps_s[:, :, :].bitcast(F16)
        att_acc = ps_acc[:, :, :].rearrange("p k (b f) -> p (k b) f", b=2)
        w_out = ps_s[:, 0, :].rearrange("p (b f) -> p b f", f=D)
        w_out2 = ps_s[:, 0:2, :].rearrange("p a (b r f) -> p (a b) r f", b=2, r=2)
        prep_out = ps_s[:, 2, :].rearrange("p (b f) -> p b f", f=D)
        prep_out2 = ps_s[:, 2:4, :].rearrange("p a (b r f) -> p (a b) r f", b=2, r=2)

        names = ("params_in x_loaded stored cast_done turned adj_placed ident_ok sig_e col_ok "
                 "stats_ok rstd_ok scale_ok relu_ok sq_ok norm_ok split0_ok u_ok ut_ps ut_ok "
                 "x_adj s_done z_done exp_done ehi_done elo_done e_used acc_free "
                 "pow_in pow_ok hd_sum hd_ok agg_done agg_out w_done l_stats l_rstd l_scale "
                 "l_relu l_split ht_ps ht_out prep_done bias_in hw_out x_done root_in root_out "
                 "exp_in exp_out ln_in ln_out h2_ok v_ok v_out g_ok "
                 "split_g dve_chain pool_chain pool_chain2").split()
        S = {n: sem(n) for n in names}
        adj_in = [sem("adj_in0"), sem("adj_in1")]
        (params_in, x_loaded, stored, cast_done, turned, adj_placed, ident_ok, sig_e, col_ok,
         stats_ok, rstd_ok, scale_ok, relu_ok, sq_ok, norm_ok, split0_ok, u_ok, ut_ps, ut_ok,
         x_adj, s_done, z_done, exp_done, ehi_done, elo_done, e_used, acc_free,
         pow_in, pow_ok, hd_sum, hd_ok, agg_done, agg_out, w_done, l_stats, l_rstd, l_scale,
         l_relu, l_split, ht_ps, ht_out, prep_done, bias_in, hw_out, x_done, root_in, root_out,
         exp_in, exp_out, ln_in, ln_out, h2_ok, v_ok, v_out, g_ok,
         split_g, dve_chain, pool_chain, pool_chain2) = (S[n] for n in names)

        adj_rows = adj.rearrange("(c p t) n -> p c t n", p=P, t=2)
        x_view = x_in.rearrange("(c p t) f -> p c t f", p=P, t=2)
        out_view = out.rearrange("(c p t) f -> p c t f", p=P, t=2)
        N_PARAMS = 12

        def parts_of(buf):
            return h_c if buf else h_a[:, :, :, 0:D]

        def pairs(ap):
            return ap.rearrange("p (c t) f -> p c t f", t=2)

        block = ctx.enter_context(nc.Block())

        @block.sync
        def _(sp):
            for s, n in ((cast_done, 2), (turned, 2), (adj_placed, 2), (exp_done, RING),
                         (elo_done, RING), (e_used, RING), (acc_free, 1), (w_done, 1),
                         (l_split, 1)):
                sp.sem_inc(s, n)
            sp.dma_start(x[:, :, :].rearrange("p (c t) f -> p c t f", t=2), x_view
                         ).then_inc(x_loaded, 16)
            with sp.Fori(0, NCH) as i:
                for m in range(HPC):
                    hh, b = m // BC, m % BC
                    sp.wait_ge(cast_done, HPC * i + m + 1)
                    sp.dma_start(stage[:, m % 2, :],
                                 adj_rows[:, ds(2 * i + b // 2, 1), b % 2, hh * HALF:(hh + 1) * HALF]
                                 .rearrange("p a n -> p (a n)")).then_inc(adj_in[m % 2], 16)
            with sp.Fori(0, NCH) as m:
                sp.wait_ge(x_done, m + 1)
                sp.dma_start(out_view[:, ds(2 * m, 2), :, :], pairs(x[:, ds(BC * m, BC), :])
                             ).then_inc(stored, 16)
            sp.wait_ge(stored, 16 * NCH)

        @block.gpsimd
        def _(pool):
            g = nc.gpsimd
            g.memset(ident16[:, :], 0.0).then_inc(ident_ok, 1)
            g.memset(ident16x2[:, :], 0.0).then_inc(ident_ok, 1)
            g.memset(ident32, 0.0).then_inc(ident_ok, 1)
            pool.wait_ge(ident_ok, 3)
            for m, v in ((ident16[:, :], 1.0), (ident16x2[:, :], A_VALUE), (ident32, 1.0)):
                g.affine_select(out=m, in_=m, compare_op=ALU.not_equal, fill=v, base=0,
                                pattern=[[-1, P]], channel_multiplier=1).then_inc(ident_ok, 1)
            g.memset(neg_half, -0.5).then_inc(ident_ok, 1)
            g.memset(half, 0.5).then_inc(ident_ok, 1)
            g.memset(h_a[:, :, LO, D:D + 2], 0.0).then_inc(ident_ok, 1)
            g.memset(h_a[:, :, HI, D:D + 2], 1.0).then_inc(ident_ok, 1)
            pool.wait_ge(ident_ok, 10)

            def power(col, e):
                return g.tensor_tensor(col, col, e.broadcast_to(col.shape), ALU.pow)

            pool.wait_ge(stats_ok, 1)
            power(rs0, neg_half).then_inc(rstd_ok, 1)
            with pool.Fori(0, NCH) as q:
                pool.wait_ge(relu_ok, q + 1)
                pool.sem_inc(pool_chain, 1)
                src = h0f[:, ds(2 * q, 2), :, :]
                dst = h_a[:, ds(BC * q, BC), :, 0:D].rearrange("p (c t) r f -> p c t r f", t=2)
                Chain(pool, pool_chain, q).step(g.tensor_copy(dst[:, :, :, HI, :], src))
                g.tensor_tensor(dst[:, :, :, LO, :], src, dst[:, :, :, HI, :], ALU.subtract
                                ).then_inc(split0_ok, 1)
            pool.wait_ge(sq_ok, 1)
            g.tensor_tensor(norm0, sq_h, half.broadcast_to([P, NB]), ALU.pow).then_inc(norm_ok, 1)

            def low_part(s, base):
                pool.wait_ge(ehi_done, base + s + 1)
                g.tensor_tensor(e_parts[:, LO, s % RING, :], ez[:, s % RING, :],
                                e_parts[:, HI, s % RING, :], ALU.subtract).then_inc(elo_done, 1)

            with pool.Fori(0, NCH - 1) as i:
                for s in range(NB):
                    low_part(s, NB * i)
            for s in range(NB):
                low_part(s, NB * (NCH - 1))
                if s == 2:
                    pool.wait_ge(pow_in, 1)
                    power(dis, neg_half).then_inc(pow_ok, 1)
                    power(d2, neg_half).then_inc(pow_ok, 1)
                if s >= 8 and s % 3 == 2 and (s - 8) // 3 < NCH:
                    m = (s - 8) // 3
                    pool.wait_ge(hd_sum, m + 1)
                    src = hd_f[:, m % 2, :].rearrange("p (b f) -> p b f", f=D)
                    dst = h_c[:, BC * m:BC * m + BC, :, :]
                    Chain(pool, pool_chain, NCH + m).step(g.tensor_copy(dst[:, :, HI, :], src))
                    g.tensor_tensor(dst[:, :, LO, :], src, dst[:, :, HI, :], ALU.subtract
                                    ).then_inc(hd_ok, 1)

            for L in range(3):
                with pool.Fori(0, NCH) as m:
                    at = NCH * L + m
                    pool.wait_ge(l_stats, at + 1)
                    power(ve, neg_half).then_inc(l_rstd, 1)
                    pool.wait_ge(l_relu, at + 1)
                    pool.sem_inc(pool_chain, 1)
                    dst = hs if L == 2 else parts_of(L % 2)[:, ds(BC * m, BC), :, :]
                    Chain(pool, pool_chain, 2 * NCH + at).step(g.tensor_copy(dst[:, :, HI, :], hf))
                    g.tensor_tensor(dst[:, :, LO, :], hf, dst[:, :, HI, :], ALU.subtract
                                    ).then_inc(l_split, 1)
                    if L == 0:
                        g.tensor_tensor(x[:, ds(BC * m, BC), :], x[:, ds(BC * m, BC), :],
                                        l1_bias_bc.unsqueeze(1).broadcast_to([P, BC, D]), ALU.add
                                        ).then_inc(bias_in, 1)
                    if L == 2:
                        for k, (src, dst) in enumerate(((sq_h[:, ds(BC * m, BC)], n_h), (v_sq, n_v),
                                                        (h2_sq, n_h2))):
                            pool.wait_ge(root_in, 3 * m + k + 1)
                            g.tensor_tensor(dst, src, half.broadcast_to([P, BC]), ALU.pow
                                            ).then_inc(root_out, 1)
                        pool.wait_ge(g_ok, m + 1)
                        pool.sem_inc(pool_chain, 1)
                        dst = parts_of(0)[:, ds(BC * m, BC), :, :]
                        Chain(pool, pool_chain2, m).step(g.tensor_copy(dst[:, :, HI, :], g_f))
                        g.tensor_tensor(dst[:, :, LO, :], g_f, dst[:, :, HI, :], ALU.subtract
                                        ).then_inc(split_g, 1)
            with pool.Fori(0, NCH) as m:
                for k, (src, dst) in enumerate(((a_sq, n_a), (cat_sq, n_cat), (v_sq, n_v))):
                    pool.wait_ge(root_in, 3 * NCH + 3 * m + k + 1)
                    g.tensor_tensor(dst, src, half.broadcast_to([P, BC]), ALU.pow
                                    ).then_inc(root_out, 1)

        @block.scalar
        def _(act):
            a = nc.scalar
            one = lambda v: v.rearrange("(a n) -> a n", a=1).broadcast_to([P, v.shape[0]])
            for dst, src in ((alpha_c, one(alpha)), (beta_c, one(beta)),
                             (kernel_sb[:, :], l1_kernel), (w_sb[:, :], l2_w),
                             (embed_top[:, 0, :], embed), (embed_top[:, 1, :], layer[0:D, :]),
                             (bot_ident[:, 0, :], layer[D:2 * D, :]),
                             (l1_bias_bc, one(l1_bias)), (l2_b_bc, one(l2_b)),
                             (eb_bc, one(embed_bias)), (lb_bc, one(layer_bias))):
                act.dma_start(dst, src).then_inc(params_in, 16)
            act.dma_start(l1b.rearrange("p (c t) -> p c t", t=2),
                          l1_beta.rearrange("(c p t) -> p c t", p=P, t=2)).then_inc(params_in, 16)
            act.wait_ge(params_in, 16 * N_PARAMS)
            a.activation(e_alpha, alpha_c, ACT.Exp, scale=-1.0).then_inc(sig_e, 1)

            def cast_quarter(i, m, r):
                hh, b = m // BC, m % BC
                if r == 0:
                    act.wait_ge(adj_in[m % 2], (HPC // 2 * i + m // 2 + 1) * 16)
                    act.wait_ge(turned, HPC * i + m + 1)
                cut = slice(HALF // 2 * r, HALF // 2 * (r + 1))
                last = a.activation(bytes8[:, m % 2, cut], stage[:, m % 2, cut], ACT.Copy,
                                    scale=A_BYTE,
                                    accum_out=deg_parts[:, ds(BC * i + b, 1), 2 * hh + r])
                if r:
                    last.then_inc(cast_done, 1)

            def cast_half(i, m):
                for r in range(2):
                    cast_quarter(i, m, r)

            act.wait_ge(scale_ok, 1)
            for q in range(NCH):
                for b in range(BC):
                    k = BC * q + b
                    last = a.activation(h0f[:, k // 2, k % 2, :], x[:, k, :], ACT.Relu,
                                        bias=nb0[:, k:k + 1], scale=rs0[:, k:k + 1])
                last.then_inc(relu_ok, 1)
                act.drain()
                for b in range(BC):
                    k = BC * q + b
                    last = a.activation(act_junk[:, b, :], h0f[:, k // 2, k % 2, :], ACT.Square,
                                        scale=1.0 / H_SCALE, accum_out=sq_h[:, k:k + 1])
                if q % 2:
                    cast_half(0, q // 2)
            last.then_inc(sq_ok, 1)
            for m in range(HPC // 2, HPC):
                cast_half(0, m)

            def exp_step(s, base):
                act.wait_ge(z_done, base + s + 1)
                act.wait_ge(elo_done, base + s + 1)
                a.activation(ez[:, s % RING, :], ps_s[:, s % RING, :], ACT.Exp, scale=beta_s,
                             bias=shift_c).then_inc(exp_done, 1)

            act.wait_ge(col_ok, 1)
            with act.Fori(0, NCH - 1) as i:
                for s in range(NB):
                    exp_step(s, NB * i)
                    if s in CAST_AT:
                        m = CAST_AT.index(s)
                        cast_quarter(i + 1, m // 2, m % 2)
            for s in range(NB):
                exp_step(s, NB * (NCH - 1))

            def squares(src, dst, ready, count):
                act.drain()
                act.wait_ge(ready, count)
                for b in range(BC):
                    last = a.activation(act_junk[:, b, :], src[:, b, :], ACT.Square,
                                        accum_out=dst[:, b:b + 1])
                return last

            def ln_step(k, src, dst):
                act.wait_ge(ln_in, k)
                a.activation(dst, src, ACT.Ln).then_inc(ln_out, 1)

            def exp_small(k):
                act.wait_ge(exp_in, k)
                a.activation(th_u, th_n, ACT.Exp).then_inc(exp_out, 1)

            for L in range(4):
                with act.Fori(0, NCH // 2) as i:
                    for par in range(2):
                        m = 2 * i + par
                        at = NCH * L + m
                        act.wait_ge(agg_done, at + 1)
                        act.wait_ge(w_done, at + 1)
                        a.activation(agg_sb, ps_acc[:, par, :], ACT.Copy,
                                     scale=1.0 / (H_SCALE * A_VALUE)).then_inc(agg_out, 1)
                        if L < 3:
                            act.wait_ge(l_scale, at + 1)
                            act.wait_ge(l_split, at + 1)
                            for b in range(BC):
                                last = a.activation(hf[:, b, :], x[:, ds(BC * m + b, 1), :]
                                                    .rearrange("p a f -> p (a f)"), ACT.Relu,
                                                    bias=nb[:, b:b + 1], scale=rs[:, b:b + 1])
                            last.then_inc(l_relu, 1)
                        if L == 0 or L == 2:
                            p_at = NCH * (L // 2) + m
                            if L == 2:
                                act.drain()
                                for b in range(BC):
                                    last = a.activation(act_junk[:, b, :], hf[:, b, :], ACT.Square,
                                                        scale=1.0 / H_SCALE,
                                                        accum_out=sq_h[:, ds(BC * m + b, 1)])
                                last.then_inc(root_in, 1)
                            act.wait_ge(ht_ps, p_at + 1)
                            a.activation(ht_sb, ps_t[:, 0, :], ACT.Copy, scale=1.0 / H_SCALE
                                         ).then_inc(ht_out, 1)
                        if L == 2:
                            ln_step(3 * m + 1, at_u, at_l)
                            act.wait_ge(prep_done, NCH + m + 1)
                            a.activation(v0, prep_out2[:, :, 0, :], ACT.Copy).then_inc(v_out, 1)
                            squares(v0, v_sq, v_out, m + 1).then_inc(root_in, 1)
                            a.activation(hw[:, ds(BC * m, BC), :], prep_out2[:, :, 1, :], ACT.Copy
                                         ).then_inc(hw_out, 1)
                            exp_small(m + 1)
                            ln_step(3 * m + 2, th_u, th_l)
                            squares(g_f, h2_sq, h2_ok, m + 1).then_inc(root_in, 1)
                            ln_step(3 * m + 3, at_u, at_l)
                        if L == 3:
                            squares(w_out2[:, :, 1, :], a_sq, w_done, at + 2).then_inc(root_in, 1)
                            exp_small(NCH + 2 * m + 1)
                            ln_step(3 * NCH + 3 * m + 1, th_u, th_l)
                            squares(v0, v_sq, v_ok, m + 1).then_inc(root_in, 1)
                            ln_step(3 * NCH + 3 * m + 2, at_u, at_l)
                            exp_small(NCH + 2 * m + 2)
                            ln_step(3 * NCH + 3 * m + 3, th_u, th_l)

        @block.vector
        def _(dve):
            v = nc.vector
            dve.wait_ge(x_loaded, 16)
            with dve.Fori(0, NCH) as q:
                for b in range(BC):
                    last = v.bn_stats(st[:, b, :], x[:, ds(BC * q + b, 1), :]
                                      .rearrange("p a f -> p (a f)"))
                c = Chain(dve, dve_chain, 2 * q)
                c.step(last)
                for b in range(BC):
                    last = v.bn_aggr(mv[:, b, :], st[:, b, :])
                c.step(last)
                c.step(v.tensor_copy(mv0[:, ds(BC * q, BC), :], mv[:, :, :]))
            ch = Chain(dve, dve_chain, 2 * NCH)
            v.tensor_scalar(rs0, mv0[:, :, 1], LN_EPS, None, ALU.add).then_inc(stats_ok, 1)
            dve.wait_ge(rstd_ok, 1)
            ch.step(v.tensor_scalar(rs0, rs0, H_SCALE, None, ALU.mult))
            v.scalar_tensor_tensor(nb0, mv0[:, :, 0], -1.0, rs0, ALU.mult, ALU.mult
                                   ).then_inc(scale_ok, 1)
            dve.wait_ge(params_in, 16 * N_PARAMS)
            dve.wait_ge(sig_e, 1)
            ch.step(v.tensor_scalar(sig_c, e_alpha, 1.0, None, ALU.add))
            ch.step(v.reciprocal(sig_c, sig_c))
            v.tensor_scalar(sig_h, sig_c, 1.0 / H_SCALE, None, ALU.mult)
            ch.step(v.tensor_scalar(x_coef, sig_c, 1.0, -1.0 / H_SCALE, ALU.add, ALU.mult))
            v.tensor_scalar(beta_s, beta_c, 1.0 / (U_SCALE * U_SCALE * A_BYTE), None, ALU.mult)
            ch.step(v.tensor_scalar(shift_c, beta_c, 0.0, -1.0, ALU.max, ALU.mult))
            v.tensor_scalar(shift_c, shift_c, E_SHIFT, None, ALU.add).then_inc(col_ok, 1)
            for n, (y, y2) in enumerate(((eb_bc, y2_embed), (lb_bc, y2_layer))):
                ch.step(v.scalar_tensor_tensor(g_f[:, n, :], y, 1.0, y, ALU.mult, ALU.mult,
                                               accum_out=y2))
            dve.wait_ge(norm_ok, 1)
            ch.step(v.tensor_scalar(run0, norm0, COS_EPS, None, ALU.max))
            ch.step(v.reciprocal(run0, run0))
            ch.step(v.tensor_scalar(run0, run0, U_SCALE / H_SCALE, None, ALU.mult))
            run_pairs = run0.rearrange("p (c t) -> p c t", t=2)

            def place(m, col, n):
                hh = m // BC
                dve.wait_ge(turned, n + 3)
                v.tensor_copy(adj_t[:, TPH * hh:TPH * (hh + 1), col],
                              ps_t16[:, m % 2, :].bitcast(U16).rearrange("p (c i) -> p c i", i=P)
                              ).then_inc(adj_placed, 1)

            def put_ut(q):
                dve.wait_ge(ut_ps, q + 1)
                v.tensor_copy(u_t[:, :, CW * q:CW * (q + 1)],
                              ps_s16[:, q % 4, :].rearrange("p (r i) -> p r i", r=2)
                              ).then_inc(ut_ok, 1)

            for q in range(NCH):
                hq, uq, up = h0f[:, 2 * q:2 * q + 2], u0f[:, 2 * q:2 * q + 2], u0p[:, 2 * q:2 * q + 2]
                ch.step(v.tensor_tensor(uq, hq, run_pairs[:, 2 * q:2 * q + 2, :].unsqueeze(3)
                                        .broadcast_to([P, 2, 2, D]), ALU.mult))
                ch.step(v.tensor_copy(up[:, :, :, HI, :], uq))
                v.tensor_tensor(up[:, :, :, LO, :], uq, up[:, :, :, HI, :], ALU.subtract
                                ).then_inc(u_ok, 1)
                v.scalar_tensor_tensor(pairs(x[:, BC * q:BC * (q + 1), :]), hq, x_coef,
                                       pairs(x[:, BC * q:BC * (q + 1), :]), ALU.mult, ALU.add)
                place(q, slice(P * (q % BC), P * (q % BC + 1)), q)
                if q:
                    put_ut(q - 1)
            put_ut(NCH - 1)

            def z_step(s, base, col, chunk):
                if s % NB == 0:
                    dve.wait_ge(adj_placed, HPC * (chunk + 1) + 2)
                dve.wait_ge(s_done, base + s + 1)
                k = s % NB
                v.tensor_tensor(ps_s[:, s % RING, :], ps_s[:, s % RING, :],
                                adj_u8[:, k // 2, col, k % 2], ALU.mult).then_inc(z_done, 1)

            def high_part(s, base):
                dve.wait_ge(exp_done, base + s + RING + 1)
                dve.wait_ge(e_used, base + s + 1)
                v.tensor_copy(e_parts[:, HI, s % RING, :], ez[:, s % RING, :]
                              ).then_inc(ehi_done, 1)

            def att_tail(i, c):
                dve.wait_ge(e_used, NB * (i + 1) + RING)
                c.step(v.reciprocal(rec, att_acc[:, :, D]))
                c.step(v.tensor_scalar(rec, rec, sig_h, None, ALU.mult))
                for b in range(BC):
                    xb = x[:, ds(BC * i + b, 1), :].rearrange("p a f -> p (a f)")
                    last = v.scalar_tensor_tensor(xb, att_acc[:, b, 0:D], rec[:, b:b + 1], xb,
                                                  ALU.mult, ALU.add)
                last.then_inc(acc_free, 1)

            n_chain = ch.base + ch.n
            for s in range(Z_AHEAD):
                z_step(s, 0, slice(0, CW), 0)
            with dve.Fori(0, NCH - 1) as i:
                for s in range(NB):
                    z_s = s + Z_AHEAD
                    if s in PLACE_AT:
                        m = PLACE_AT.index(s)
                        place(m, ds(CW * (i + 1) + P * (m % BC), P), HPC * (i + 1) + m)
                    z_step(z_s, NB * i, ds(CW * (i + z_s // NB), CW), i + z_s // NB)
                    high_part(s, NB * i)
                att_tail(i, Chain(dve, dve_chain, n_chain + 2 * i))
            ch = Chain(dve, dve_chain, n_chain + 2 * (NCH - 1))
            for s in range(NB):
                if s + Z_AHEAD < NB:
                    z_step(s + Z_AHEAD, NB * (NCH - 1), slice(CW * (NCH - 1), N), NCH - 1)
                high_part(s, NB * (NCH - 1))
                if s == 0:
                    dve.wait_ge(cast_done, HPC * NCH + 2)
                    ch.step(v.tensor_reduce(deg, deg_parts[:, :, :], mybir.AxisListType.X, ALU.add))
                    ch.step(v.tensor_scalar(deg, deg, 1.0 / A_BYTE, None, ALU.mult))
                    v.tensor_scalar(dis, deg, 1.0, None, ALU.max)
                    v.tensor_tensor(inv_deg, deg, l1b, ALU.add)
                    v.tensor_scalar(d2, deg, 1.0, None, ALU.add).then_inc(pow_in, 1)
                    dve.wait_ge(pow_in, 1)
                    ch.step(v.reciprocal(inv_deg, inv_deg))
                    ch.step(v.tensor_tensor(inv_beta, inv_deg, l1b, ALU.mult))
                if s >= 7 and s % 3 == 1 and (s - 7) // 3 < NCH:
                    m = (s - 7) // 3
                    if m == 0:
                        dve.wait_ge(pow_ok, 2)
                    if m >= 2:
                        dve.wait_ge(hd_ok, m - 1)
                    dst = hd_f[:, m % 2, :].rearrange("p (b f) -> p b f", f=D)
                    hm = h_a[:, BC * m:BC * m + BC, :, 0:D]
                    ch.step(v.tensor_tensor(dst, hm[:, :, HI, :], hm[:, :, LO, :], ALU.add))
                    v.tensor_tensor(dst, dst, dis[:, BC * m:BC * m + BC].unsqueeze(2)
                                    .broadcast_to([P, BC, D]), ALU.mult).then_inc(hd_sum, 1)
            att_tail(NCH - 1, ch)
            n_chain = ch.base + ch.n

            def layer_norm(c, L, m, at):
                for b in range(BC):
                    last = v.bn_stats(st[:, b, :], x[:, ds(BC * m + b, 1), :]
                                      .rearrange("p a f -> p (a f)"))
                c.step(last)
                for b in range(BC):
                    last = v.bn_aggr(mv[:, b, :], st[:, b, :])
                c.step(last)
                v.tensor_scalar(ve, mv[:, :, 1], LN_EPS, None, ALU.add).then_inc(l_stats, 1)
                dve.wait_ge(l_rstd, at + 1)
                if L == 1:
                    c.step(v.scalar_tensor_tensor(rs, ve, H_SCALE, d2[:, ds(BC * m, BC)],
                                                  ALU.mult, ALU.mult))
                else:
                    c.step(v.tensor_scalar(rs, ve, H_SCALE, None, ALU.mult))
                v.scalar_tensor_tensor(nb, mv[:, :, 0], -1.0, rs, ALU.mult, ALU.mult
                                       ).then_inc(l_scale, 1)

            def atanh_over_n(c, n, dst, factor, k):
                c.step(v.tensor_scalar(at_n, n, MAX_TANH, None, ALU.min))
                c.step(v.tensor_scalar(at_o, at_n, -1.0, 1.0, ALU.mult, ALU.add))
                c.step(v.reciprocal(at_o, at_o))
                c.step(v.scalar_tensor_tensor(at_t, at_n, 2.0, at_o, ALU.mult, ALU.mult))
                v.tensor_scalar(at_u, at_t, 1.0, None, ALU.add).then_inc(ln_in, 1)
                dve.wait_ge(ln_in, k)
                c.step(v.scalar_tensor_tensor(at_w, at_u, -1.0, n, ALU.add, ALU.mult))
                c.step(v.reciprocal(at_w, at_w))
                dve.wait_ge(ln_out, k)
                c.step(v.scalar_tensor_tensor(at_t, at_t, 0.5 * factor, at_l, ALU.mult, ALU.mult))
                c.step(v.tensor_tensor(dst, at_t, at_w, ALU.mult))

            def tanh_of(c, n, k_exp, k_ln):
                v.tensor_scalar(th_n, n, 20.0, 2.0, ALU.min, ALU.mult).then_inc(exp_in, 1)
                dve.wait_ge(exp_out, k_exp)
                v.tensor_scalar(th_u, th_u, NEXT_AFTER_1, None, ALU.max).then_inc(ln_in, 1)
                dve.wait_ge(ln_in, k_ln)
                c.step(v.scalar_tensor_tensor(th_w, th_u, -1.0, th_n, ALU.add, ALU.mult))
                dve.wait_ge(ln_out, k_ln)
                c.step(v.reciprocal(th_l, th_l))
                c.step(v.tensor_tensor(th_w, th_w, th_l, ALU.mult))
                c.step(v.tensor_scalar(th, th_w, 2.0, None, ALU.add))
                c.step(v.reciprocal(th, th))
                c.step(v.tensor_tensor(th, th, th_w, ALU.mult))

            def exp_map_add(c, scale, w, y, y2, k_root, k_exp, k_ln):
                for b in range(BC):
                    last = v.scalar_tensor_tensor(dve_junk[:, b, :], w[:, b, :], 1.0, y, ALU.mult, ALU.mult,
                                                  accum_out=v_y[:, b:b + 1])
                c.step(last)
                dve.wait_ge(root_out, k_root)
                c.step(v.tensor_tensor(n_v, n_v, scale, ALU.mult))
                c.step(v.tensor_scalar(n_v, n_v, EPS, None, ALU.max))
                tanh_of(c, n_v, k_exp, k_ln)
                c.step(v.reciprocal(n_v, n_v))
                c.step(v.tensor_tensor(q_c, th, n_v, ALU.mult))
                c.step(v.tensor_tensor(q_c, q_c, scale, ALU.mult))
                c.step(v.tensor_tensor(v_y, v_y, q_c, ALU.mult))
                c.step(v.tensor_tensor(x2, v_sq, q_c, ALU.mult))
                c.step(v.tensor_tensor(x2, x2, q_c, ALU.mult))
                c.step(v.tensor_scalar(a_c, v_y, 2.0, 1.0, ALU.mult, ALU.add))
                c.step(v.scalar_tensor_tensor(b_c, x2, y2, a_c, ALU.mult, ALU.add))
                c.step(v.tensor_scalar(b_c, b_c, EPS, None, ALU.max))
                c.step(v.reciprocal(b_c, b_c))
                c.step(v.scalar_tensor_tensor(a_c, a_c, y2, q_c, ALU.add, ALU.mult))
                c.step(v.tensor_tensor(a_c, a_c, b_c, ALU.mult))
                c.step(v.tensor_scalar(x2, x2, -1.0, 1.0, ALU.mult, ALU.add))
                c.step(v.tensor_tensor(b_c, b_c, x2, ALU.mult))

            for L in range(3):
                links = LINKS[L]
                with dve.Fori(0, NCH) as m:
                    at = NCH * L + m
                    c = Chain(dve, dve_chain, n_chain + links * m)
                    dve.wait_ge(w_done, at + 2)
                    xc = x[:, ds(BC * m, BC), :]
                    if L == 2:
                        for b in range(BC):
                            last = v.scalar_tensor_tensor(tmp[:, b, :], w_out[:, b, :],
                                                          d2[:, ds(BC * m + b, 1)], l2_b_bc,
                                                          ALU.mult, ALU.add)
                        c.step(last)
                        c.step(v.scalar_tensor_tensor(xc, tmp, 0.0, xc, ALU.max, ALU.add))
                    else:
                        col = dis if L == 0 else inv_deg
                        for b in range(BC):
                            xb = x[:, ds(BC * m + b, 1), :].rearrange("p a f -> p (a f)")
                            last = v.scalar_tensor_tensor(xb, w_out[:, b, :],
                                                          col[:, ds(BC * m + b, 1)], xb,
                                                          ALU.mult, ALU.add)
                        c.step(last)
                    layer_norm(c, L, m, at)
                    if L == 0:
                        dve.wait_ge(prep_done, m + 1)
                        dve.wait_ge(bias_in, m + 1)
                        for b in range(BC):
                            xb = x[:, ds(BC * m + b, 1), :].rearrange("p a f -> p (a f)")
                            last = v.scalar_tensor_tensor(xb, prep_out[:, b, :],
                                                          inv_beta[:, ds(BC * m + b, 1)], xb,
                                                          ALU.mult, ALU.add)
                        c.step(last)
                    if L == 2:
                        dve.wait_ge(root_out, 3 * m + 1)
                        c.step(v.tensor_scalar(n_h, n_h, EPS, None, ALU.max))
                        atanh_over_n(c, n_h, l_h, 1.0, 3 * m + 1)
                        dve.wait_ge(v_out, m + 1)
                        w = v0
                        exp_map_add(c, l_h, w, eb_bc, y2_embed, 3 * m + 2, m + 1, 3 * m + 2)
                        for b in range(BC):
                            last = v.tensor_scalar(tmp[:, b, :], eb_bc, b_c[:, b:b + 1], None,
                                                   ALU.mult)
                        c.step(last)
                        for b in range(BC):
                            last = v.scalar_tensor_tensor(g_f[:, b, :], w[:, b, :],
                                                          a_c[:, b:b + 1], tmp[:, b, :],
                                                          ALU.mult, ALU.add)
                        last.then_inc(h2_ok, 1)
                        dve.wait_ge(root_out, 3 * m + 3)
                        c.step(v.tensor_scalar(n_h2, n_h2, EPS, None, ALU.max))
                        atanh_over_n(c, n_h2, l_h, H_SCALE, 3 * m + 3)
                        for b in range(BC):
                            last = v.tensor_scalar(g_f[:, b, :], g_f[:, b, :], l_h[:, b:b + 1],
                                                   None, ALU.mult)
                        last.then_inc(g_ok, 1)
                    assert c.n == links, (L, c.n)
                n_chain = n_chain + links * NCH

            with dve.Fori(0, NCH) as m:
                c = Chain(dve, dve_chain, n_chain + LINKS[3] * m)
                at = 3 * NCH + m
                dve.wait_ge(root_out, 3 * NCH + 3 * m + 1)
                c.step(v.tensor_scalar(n_a, n_a, EPS, None, ALU.max))
                tanh_of(c, n_a, NCH + 2 * m + 1, 3 * NCH + 3 * m + 1)
                c.step(v.reciprocal(n_a, n_a))
                c.step(v.tensor_tensor(tq, th, n_a, ALU.mult))
                c.step(v.tensor_tensor(cat_sq, tq, tq, ALU.mult))
                c.step(v.tensor_tensor(cat_sq, cat_sq, a_sq, ALU.mult))
                v.tensor_tensor(cat_sq, cat_sq, sq_h[:, ds(BC * m, BC)], ALU.add
                                ).then_inc(root_in, 1)
                for b in range(BC):
                    last = v.scalar_tensor_tensor(v0[:, b, :], w_out2[:, b, 0, :], tq[:, b:b + 1],
                                                  hw[:, ds(BC * m + b, 1), :]
                                                  .rearrange("p a f -> p (a f)"),
                                                  ALU.mult, ALU.add)
                last.then_inc(v_ok, 1)
                dve.wait_ge(v_ok, m + 1)
                dve.wait_ge(root_out, 3 * NCH + 3 * m + 2)
                c.step(v.tensor_scalar(n_cat, n_cat, EPS, None, ALU.max))
                atanh_over_n(c, n_cat, l_cat, 1.0, 3 * NCH + 3 * m + 2)
                exp_map_add(c, l_cat, v0, lb_bc, y2_layer, 3 * NCH + 3 * m + 3, NCH + 2 * m + 2,
                            3 * NCH + 3 * m + 3)
                for b in range(BC):
                    xb = x[:, ds(BC * m + b, 1), :].rearrange("p a f -> p (a f)")
                    last = v.scalar_tensor_tensor(xb, lb_bc, b_c[:, b:b + 1], xb, ALU.mult, ALU.add)
                c.step(last)
                for b in range(BC):
                    xb = x[:, ds(BC * m + b, 1), :].rearrange("p a f -> p (a f)")
                    last = v.scalar_tensor_tensor(xb, v0[:, b, :], a_c[:, b:b + 1], xb,
                                                  ALU.mult, ALU.add)
                last.then_inc(x_done, 1)
                assert c.n == LINKS[3], c.n

        @block.tensor
        def _(pe):
            t = nc.tensor
            pe.wait_ge(ident_ok, 10)

            def turn(m, half_no):
                pe.wait_ge(cast_done, half_no + 3)
                pe.wait_ge(adj_placed, half_no + 1)
                src = bytes8[:, m % 2, :].bitcast(F16)
                for c in range(TPH):
                    last = t.transpose(ps_t16[:, m % 2, P * c:P * (c + 1)],
                                       src[:, P * c:P * (c + 1)], ident16[:, :])
                last.then_inc(turned, 1)

            turn(0, 0)
            turn(1, 1)
            for q in range(NCH):
                pe.wait_ge(u_ok, q + 1)
                if q >= 4:
                    pe.wait_ge(ut_ok, q - 3)
                dst = ps_s16[:, q % 4, :].rearrange("p (r i) -> p r i", r=2)
                for k in range(BC * q, BC * (q + 1)):
                    for r in (LO, HI):
                        last = t.transpose(dst[:, r, P * (k % BC):P * (k % BC + 1)],
                                           u0p[:, k // 2, k % 2, r, :], ident16[:, :])
                last.then_inc(ut_ps, 1)
                if q + 2 < HPC:
                    turn(q + 2, q + 2)
            pe.wait_ge(ut_ok, NCH)

            def scores(s, base, col):
                pe.wait_ge(exp_done, base + s + 1)
                k = s % NB
                for n, (rj, ri) in enumerate(((HI, HI), (HI, LO), (LO, HI))):
                    last = t.matmul(ps_s[:, s % RING, :], u_t[:, rj, P * k:P * (k + 1)],
                                    u_t[:, ri, col], start=(n == 0), stop=(n == 2))
                last.then_inc(s_done, 1)

            def att_products(s, base):
                pe.wait_ge(elo_done, base + s + RING + 1)
                for b in range(BC):
                    for n, (re, rh) in enumerate(((HI, HI), (HI, LO), (LO, HI))):
                        last = t.matmul(att_acc[:, b, 0:D + 1],
                                        e_parts[:, re, s % RING, P * b:P * (b + 1)],
                                        h_a[:, s, rh, 0:D + 1],
                                        start=(s == 0 and n == 0 and b % 2 == 0),
                                        stop=(s == NB - 1 and n == 2),
                                        skip_group_check=True)
                return last

            pe.wait_ge(split0_ok, NCH)
            for s in range(RING):
                scores(s, 0, slice(0, CW))
            with pe.Fori(0, NCH - 1) as i:
                for s in range(NB):
                    if s in TURN_AT:
                        m = TURN_AT.index(s)
                        turn(m, HPC * (i + 1) + m)
                    s_s = s + RING
                    scores(s_s, NB * i, ds(CW * (i + s_s // NB), CW))
                    if s == 0:
                        pe.wait_ge(acc_free, i + 1)
                    att_products(s, NB * i).then_inc(e_used, 1)
            base = NB * (NCH - 1)
            for s in range(NB):
                if s + RING < NB:
                    scores(s + RING, base, slice(CW * (NCH - 1), N))
                if s == 0:
                    pe.wait_ge(acc_free, NCH)
                att_products(s, base).then_inc(e_used, 1)

            pe.wait_ge(params_in, 16 * N_PARAMS)

            def aggregate(L, c, q):
                h = parts_of((L + 1) % 2)
                acc = ps_acc[:, c % 2, :]
                if q == 0:
                    if L == 0 and c < 2:
                        pe.wait_ge(acc_free, NCH + 1)
                    else:
                        pe.wait_ge(agg_out, NCH * L + c - 1)
                if c < 2:
                    ready, n = ((hd_ok, 0), (l_split, 1), (l_split, NCH + 1), (split_g, 0))[L]
                    pe.wait_ge(ready, n + q + 1)
                if L == 2 and q == NB // BC - 1:
                    for b in range(BC):
                        for r in (LO, HI):
                            t.matmul(acc[:, P * b:P * (b + 1)], h[:, BC * c + b, r, :],
                                     ident16x2[:, :], start=False, stop=False,
                                     skip_group_check=True)
                for k in range(BC * q, BC * (q + 1)):
                    for r in (LO, HI):
                        last = t.matmul(acc, h[:, k, r, :],
                                        adj_f8[:, k // 2, CW * c:CW * (c + 1), k % 2],
                                        start=(k == 0 and r == LO),
                                        stop=(k == NB - 1 and r == HI))
                if q == NB // BC - 1:
                    last.then_inc(agg_done, 1)

            def weights(L, m):
                at = NCH * L + m
                pe.wait_ge(agg_out, at + 1)
                if L < 3:
                    if at:
                        pe.wait_ge(l_stats, at)
                    rhs = (ident32, kernel_sb[:, :], w_sb[:, :])[L]
                    for b in range(BC):
                        last = t.matmul(w_out[:, b, :], agg_sb[:, P * b:P * (b + 1)], rhs,
                                        start=True, stop=True)
                else:
                    if m:
                        pe.wait_ge(v_ok, m)
                    else:
                        pe.wait_ge(l_stats, at)
                    for b in range(BC):
                        last = t.matmul(w_out2[:, b, :, :], agg_sb[:, P * b:P * (b + 1)],
                                        bot_ident[:, :, :], start=True, stop=True)
                last.then_inc(w_done, 1)

            def turn_h(L, m):
                pe.wait_ge(l_split, NCH * L + m + 2)
                for b in range(BC):
                    for r in (LO, HI):
                        src = hs[:, b, r, :] if L == 2 else parts_of(0)[:, BC * m + b, r, :]
                        last = t.matmul(ps_t[:, 0, P * b:P * (b + 1)], src, ident16[:, :],
                                        start=(r == LO), stop=(r == HI))
                last.then_inc(ht_ps, 1)

            def prepare(L, m):
                pe.wait_ge(ht_out, NCH * (L // 2) + m + 1)
                for b in range(BC):
                    if L == 0:
                        last = t.matmul(prep_out[:, b, :], ht_sb[:, P * b:P * (b + 1)],
                                        kernel_sb[:, :], start=True, stop=True)
                    else:
                        last = t.matmul(prep_out2[:, b, :, :], ht_sb[:, P * b:P * (b + 1)],
                                        embed_top[:, :, :], start=True, stop=True)
                last.then_inc(prep_done, 1)

            def small_steps(L, idx):
                if idx in W_AFTER:
                    weights(L, W_AFTER.index(idx))
                if L in (0, 2) and idx in T_AFTER:
                    turn_h(L, T_AFTER.index(idx))
                if L in (0, 2) and idx in V_AFTER:
                    prepare(L, V_AFTER.index(idx))

            for L in range(4):
                for idx, (c, q) in enumerate(QUARTERS):
                    aggregate(L, c, q)
                    if L:
                        small_steps(L - 1, idx + len(QUARTERS))
                    small_steps(L, idx)
            weights(3, NCH - 1)


_INS = ["x", "adj", "L0_gnn_alpha", "L0_gnn_beta", "L1_gnn_kernel", "L1_gnn_bias", "L1_gnn_beta",
        "L2_gnn_W", "L2_gnn_b", "L3_gnn_embed", "L3_gnn_layer", "L3_gnn_embed_bias",
        "L3_gnn_layer_bias"]


def kernel(**inputs):
    import numpy as np
    import concourse.bacc as bacc
    from concourse.bass_utils import run_bass_kernel_spmd

    nc = bacc.Bacc("TRN2", target_bir_lowering=False, num_devices=1, dynamic_dma_scratch_size=1024)
    arrays, args = {}, []
    for n in _INS:
        v = np.ascontiguousarray(inputs[n])
        v = v.reshape(v.shape or (1,))
        arrays[f"in_{n}"] = v
        args.append(nc.dram_tensor(f"in_{n}", v.shape, mybir.dt.from_np(v.dtype),
                                   kind="ExternalInput").ap())
    out = nc.dram_tensor("out_0", (N, D), F32, kind="ExternalOutput").ap()
    program(nc, *args, out)
    r = run_bass_kernel_spmd(nc, [arrays], core_ids=[0])
    return r.results[0]["out_0"]
```

```python
from contextlib import ExitStack

import concourse.bass as bass
from concourse import mybir

F32, F16 = mybir.dt.float32, mybir.dt.float16
U8, U16, F8 = mybir.dt.uint8, mybir.dt.uint16, mybir.dt.float8e4
ALU, ACT = mybir.AluOpType, mybir.ActivationFunctionType

N, D = 4096, 128
P = 128
NB = N // P
NP = NB // 2
BC = 4
NCH = NB // BC
CW = BC * P
HALF = N // 2
HPC = 2 * BC
TPH = HALF // 2 // P
NG = 4
GB = NB // NG
RING = 4
Z_AHEAD = 1

EARLY = 2

CAST_AT = [3 * m + r for m in range(HPC) for r in (1, 2)]
TURN_AT = [3 * m + 2 for m in range(HPC)]
PLACE_AT = [3 * m + 8 for m in range(HPC)]

HD_AT = [8 + 6 * m for m in range(4)]
FILL_AT = [27, 28, 29, 30]

H_SCALE = 4096.0
U_SCALE = 16384.0
A_BYTE = 64.0
A_VALUE = 2.0
E_SHIFT = 10.0
LN_EPS, COS_EPS, EPS = 1e-5, 1e-8, 1e-7
MAX_TANH = 1.0 - 1e-6


QUARTERS = ([(0, q) for q in range(7)] + [(1, q) for q in range(7)] + [(0, 7), (1, 7)]
            + [(c, q) for c in range(2, NCH) for q in range(8)])
QUARTERS_0 = ([(c, q) for q4 in ((0, 1, 2, 3), (4, 5), (6, 7)) for c in (0, 1) for q in q4]
              + [(c, q) for c in range(2, NCH) for q in range(8)])
QUARTERS_3 = ([(c, q) for q4 in ((0, 1, 2, 3), (4, 5)) for c in (0, 1, 2) for q in q4]
              + [(3, q) for q in range(4)] + [(c, q) for c in (0, 1, 2) for q in (6, 7)]
              + [(3, q) for q in range(4, 8)]
              + [(c, q) for c in range(4, NCH) for q in range(8)])
W_0 = [15, 22, 29, 36, 43, 50, 57, 64]
W_1 = [15, 21, 27, 33, 40, 48, 56, 64]
W_AFTER = (W_0, W_1, [15, 20, 29, 35, 46, 51, 61, 67], [24, 26, 33, 35, 41, 49, 57, 64])
T_AFTER = ([w + 6 for w in W_0], (), [20, 25, 36, 41, 52, 57, 68, 73], ())
V_AFTER = tuple([t + 1 for t in ts] for ts in T_AFTER)


def program(nc, x_in, adj, alpha, beta, l1_kernel, l1_bias, l1_beta, l2_w, l2_b, embed, layer,
            embed_bias, layer_bias, out):
    ctx = ExitStack()
    with ctx:
        def sb(name, shape, dt=F32):
            return ctx.enter_context(nc.sbuf_tensor(name, shape, dt))

        def sem(name):
            return ctx.enter_context(nc.semaphore(name))

        ds = bass.ds

        adj_t = sb("adj_t", [P, NP, N], U16)
        adj_u8 = adj_t[:, :, :].bitcast(U8).rearrange("p c (i t) -> p c i t", t=2)
        adj_f8 = adj_t[:, :, :].bitcast(F8).rearrange("p c (i t) -> p c i t", t=2)
        x = sb("x", [P, NB, D])
        LO, HI = 0, 1
        h_a = sb("h_a", [P, NB, 2, D + 2], F16)
        stage = sb("stage", [P, 2, HALF])
        h_c = stage[:, :, :].rearrange("p a n -> p (a n)").bitcast(F16).rearrange(
            "p (k r f) -> p k r f", r=2, f=D)
        u_t = sb("u_t", [P, 2, N], F16)
        hw = u_t[:, :, :].rearrange("p a n -> p (a n)").bitcast(F32).rearrange(
            "p (k f) -> p k f", f=D)
        bytes8 = sb("bytes8", [P, 2, HALF], U8)
        hd_f = bytes8[:, :, :].bitcast(F32)
        ez = sb("ez", [P, RING, CW])
        e_parts = sb("e_parts", [P, 2, RING, CW], F16)
        agg_sb = ez[:, 0, :]
        hf = ez[:, 1, :].rearrange("p (b f) -> p b f", f=D)
        g_f = ez[:, 2:4, :].rearrange("p a (b f) -> p (a b) f", f=D)
        ep = e_parts[:, :, :, :].rearrange("p a r n -> p (a r n)")
        hs = ep[:, 0:2 * CW].rearrange("p (b r f) -> p b r f", r=2, f=D)
        v0 = ep[:, 2 * CW:6 * CW].bitcast(F32).rearrange("p (b f) -> p b f", f=D)
        act_junk = ep[:, 6 * CW:8 * CW].bitcast(F32).rearrange("p (b f) -> p b f", f=D)
        tmp = bytes8[:, 0, :].bitcast(F32).rearrange("p (b f) -> p b f", f=D)
        ht_sb = bytes8[:, 1, :].bitcast(F32)
        h0f = adj_t[:, :, (NCH - 1) * CW:].bitcast(F32).rearrange("p c (t f) -> p c t f", t=2)
        u0f = adj_t[:, :, 5 * CW:6 * CW].bitcast(F32).rearrange("p c (t f) -> p c t f", t=2)
        u0p = adj_t[:, :, 6 * CW:7 * CW].bitcast(F16).rearrange("p c (t r f) -> p c t r f", r=2, t=2)

        kernel_sb = sb("kernel_sb", [D, D])
        w_sb = sb("w_sb", [D, D])
        embed_top = sb("embed_top", [D, 2, D])
        bot_ident = sb("bot_ident", [D, 2, D])
        ident32 = bot_ident[:, 1, :]
        ident16 = sb("ident16", [P, P], F16)
        ident16x2 = sb("ident16x2", [P, P], F16)
        bias_bc = sb("bias_bc", [P, 4, D])
        l1_bias_bc, l2_b_bc, eb_bc, lb_bc = (bias_bc[:, n, :] for n in range(4))
        scal = sb("scal", [P, 12])
        (alpha_c, beta_c, e_alpha, sig_c, sig_h, x_coef, beta_s, shift_c, y2_embed, y2_layer,
         neg_half, half) = (scal[:, n:n + 1] for n in range(12))
        deg_parts = sb("deg_parts", [P, NB, 4])
        cols = sb("cols", [P, 11, NB])
        (deg, dis, inv_deg, inv_beta, d2, l1b, rs0, nb0, sq_h, norm0, run0) = (
            cols[:, n, :] for n in range(11))
        st = sb("st", [P, GB, 6])
        mv = sb("mv", [P, BC, 2])
        mv0 = sb("mv0", [P, NB, 2])
        small = sb("small", [P, 4, BC])
        rec, ve, rs, nb = (small[:, n, :] for n in range(4))
        PB = 2 * BC
        hyp = sb("hyp", [P, 26, PB])
        (n_h, l_h, v_sq, n_v, v_y, a_c, b_c, at_n, at_o, at_t, at_u, at_l, at_w, th_q, th,
         th_a, th_x, x2, a_sq, n_a, n_h2, cat_sq, n_cat, tq, h2_sq, r_a) = (
            hyp[:, n, :] for n in range(26))

        ps_s = ctx.enter_context(nc.psum_tensor("ps_s", [P, 4, CW], F32))
        ps_acc = ctx.enter_context(nc.psum_tensor("ps_acc", [P, 2, CW], F32))
        ps_t = ctx.enter_context(nc.psum_tensor("ps_t", [P, 2, CW], F32))
        ps_t16 = ps_t[:, :, :].bitcast(F16)
        ps_s16 = ps_s[:, :, :].bitcast(F16)
        att_acc = ps_acc[:, :, :].rearrange("p k (b f) -> p (k b) f", b=2)
        w_out = ps_s[:, 0, :].rearrange("p (b f) -> p b f", f=D)
        w_out2 = ps_s[:, :, :].rearrange("p a (b r f) -> p (a b) r f", b=2, r=2)
        prep_out = ps_s[:, 2, :].rearrange("p (b f) -> p b f", f=D)
        prep_out2 = ps_s[:, 2:4, :].rearrange("p a (b r f) -> p (a b) r f", b=2, r=2)

        names = ("params_in stored cast_done turned adj_placed ident_ok sig_e col_ok "
                 "stats_ok rstd_ok scale_ok relu_ok hi_ok sq_ok norm_ok split0_ok u_hi_ok u_ok ut_ps ut_ok "
                 "s_done z_done exp_done ehi_done elo_done e_used acc_free "
                 "pow_in pow_ok hd_sum hd_hi hd_ok agg_done agg_out w_done l_stats l_rstd l_scale "
                 "l_relu l_split ht_ps ht_out prep_done bias_in hw_out x_done h_sq_in n_h_ok v_sq_in n_v_ok "
                 "h2_sq_in n_h2_ok a_sq_in n_a_ok cat_sq_in n_cat_ok "
                 "tanh_in tanh_out ln_in ln_out h2_ok v_ok v_out "
                 "split_g").split()
        S = {n: sem(n) for n in names}
        adj_in = [sem("adj_in0"), sem("adj_in1")]
        x_loaded = [sem(f"x_loaded{n}") for n in range(NG)]
        (params_in, stored, cast_done, turned, adj_placed, ident_ok, sig_e, col_ok,
         stats_ok, rstd_ok, scale_ok, relu_ok, hi_ok, sq_ok, norm_ok, split0_ok, u_hi_ok, u_ok, ut_ps, ut_ok,
         s_done, z_done, exp_done, ehi_done, elo_done, e_used, acc_free,
         pow_in, pow_ok, hd_sum, hd_hi, hd_ok, agg_done, agg_out, w_done, l_stats, l_rstd, l_scale,
         l_relu, l_split, ht_ps, ht_out, prep_done, bias_in, hw_out, x_done, h_sq_in, n_h_ok, v_sq_in, n_v_ok,
         h2_sq_in, n_h2_ok, a_sq_in, n_a_ok, cat_sq_in, n_cat_ok,
         tanh_in, tanh_out, ln_in, ln_out, h2_ok, v_ok, v_out,
         split_g) = (S[n] for n in names)

        adj_rows = adj.rearrange("(c p t) n -> p c t n", p=P, t=2)
        x_view = x_in.rearrange("(c p t) f -> p c t f", p=P, t=2)
        out_view = out.rearrange("(c p t) f -> p c t f", p=P, t=2)
        N_PARAMS = 12

        def parts_of(buf):
            return h_c if buf else h_a[:, :, :, 0:D]

        def hd_of(m):
            return hd_f[:, m % 2, :].rearrange("p (b f) -> p b f", f=D)

        def pairs(ap):
            return ap.rearrange("p (c t) f -> p c t f", t=2)

        block = ctx.enter_context(nc.Block())

        @block.sync
        def _(sp):
            for s, n in ((cast_done, 2), (turned, 2), (adj_placed, 2), (exp_done, RING),
                         (elo_done, RING), (e_used, RING), (acc_free, 2), (w_done, 1),
                         (l_split, 1)):
                sp.sem_inc(s, n)
            for n in range(NG):
                sp.dma_start(x[:, GB * n:GB * (n + 1), :].rearrange("p (c t) f -> p c t f", t=2),
                             x_view[:, GB // 2 * n:GB // 2 * (n + 1), :, :]
                             ).then_inc(x_loaded[n], 16)
            with sp.Fori(0, NCH) as i:
                for m in range(HPC):
                    hh, b = m // BC, m % BC
                    sp.wait_ge(cast_done, HPC * i + m + 1)
                    sp.dma_start(stage[:, m % 2, :],
                                 adj_rows[:, ds(2 * i + b // 2, 1), b % 2, hh * HALF:(hh + 1) * HALF]
                                 .rearrange("p a n -> p (a n)")).then_inc(adj_in[m % 2], 16)
            with sp.Fori(0, NCH) as m:
                sp.wait_ge(x_done, m + 1)
                sp.dma_start(out_view[:, ds(2 * m, 2), :, :], pairs(x[:, ds(BC * m, BC), :])
                             ).then_inc(stored, 16)
            sp.wait_ge(stored, 16 * NCH)

        @block.gpsimd
        def _(pool):
            g = nc.gpsimd
            g.memset(ident16[:, :], 0.0).then_inc(ident_ok, 1)
            g.memset(ident16x2[:, :], 0.0).then_inc(ident_ok, 1)
            g.memset(ident32, 0.0).then_inc(ident_ok, 1)
            pool.wait_ge(ident_ok, 3)
            for m, v in ((ident16[:, :], 1.0), (ident16x2[:, :], A_VALUE), (ident32, 1.0)):
                g.affine_select(out=m, in_=m, compare_op=ALU.not_equal, fill=v, base=0,
                                pattern=[[-1, P]], channel_multiplier=1).then_inc(ident_ok, 1)
            g.memset(neg_half, -0.5).then_inc(ident_ok, 1)
            g.memset(half, 0.5).then_inc(ident_ok, 1)
            g.memset(h_a[:, :, LO, D:D + 2], 0.0).then_inc(ident_ok, 1)
            g.memset(h_a[:, :, HI, D:D + 2], 1.0).then_inc(ident_ok, 1)
            pool.wait_ge(ident_ok, 10)

            def power(col, e):
                return g.tensor_tensor(col, col, e.broadcast_to(col.shape), ALU.pow)

            for n in range(NG):
                pool.wait_ge(stats_ok, n + 1)
                power(rs0[:, GB * n:GB * (n + 1)], neg_half).then_inc(rstd_ok, 1)

            def quarter(buf, q):
                return buf[:, 2 * q:2 * q + 2]

            def low_u(q):
                pool.wait_ge(u_hi_ok, q + 1)
                g.tensor_tensor(quarter(u0p, q)[:, :, :, LO, :], quarter(u0f, q),
                                quarter(u0p, q)[:, :, :, HI, :], ALU.subtract).then_inc(u_ok, 1)

            for n in range(NG):
                cols_n = slice(GB * n, GB * (n + 1))
                pool.wait_ge(sq_ok, n + 1)
                g.tensor_tensor(norm0[:, cols_n], sq_h[:, cols_n], half.broadcast_to([P, GB]),
                                ALU.pow).then_inc(norm_ok, 1)
                if n:
                    low_u(2 * n - 2)
                    low_u(2 * n - 1)
                for q in (2 * n, 2 * n + 1):
                    pool.wait_ge(hi_ok, q + 1)
                    dst = h_a[:, BC * q:BC * (q + 1), :, 0:D].rearrange(
                        "p (c t) r f -> p c t r f", t=2)
                    g.tensor_tensor(dst[:, :, :, LO, :], quarter(h0f, q), dst[:, :, :, HI, :],
                                    ALU.subtract).then_inc(split0_ok, 1)
            low_u(NCH - 2)
            low_u(NCH - 1)

            def low_part(s, base):
                pool.wait_ge(ehi_done, base + s + 1)
                g.tensor_tensor(e_parts[:, LO, s % RING, :], ez[:, s % RING, :],
                                e_parts[:, HI, s % RING, :], ALU.subtract).then_inc(elo_done, 1)

            def root_degree(i):
                pool.wait_ge(pow_in, i + 1)
                power(dis[:, ds(BC * i, BC)], neg_half).then_inc(pow_ok, 1)

            with pool.Fori(0, NCH - 1) as i:
                for s in range(NB):
                    low_part(s, NB * i)
                    if s == 20:
                        root_degree(i)
            for s in range(NB):
                low_part(s, NB * (NCH - 1))
                if s == 6:
                    root_degree(NCH - 1)
            pool.wait_ge(pow_in, NCH + 1)
            power(d2, neg_half).then_inc(pow_ok, 1)

            def rstd(at):
                pool.wait_ge(l_stats, at + 1)
                power(ve, neg_half).then_inc(l_rstd, 1)

            def root(src, dst, ready, done, count):
                pool.wait_ge(ready, count)
                g.tensor_tensor(dst, src, half.broadcast_to(dst.shape), ALU.pow).then_inc(done, 1)

            def of_chunk(cols, par):
                return cols[:, BC * par:BC * (par + 1)]

            with pool.Fori(0, NCH) as m:
                rstd(m)
                pool.wait_ge(l_relu, m + 1)
                g.tensor_tensor(x[:, ds(BC * m, BC), :], x[:, ds(BC * m, BC), :],
                                l1_bias_bc.unsqueeze(1).broadcast_to([P, BC, D]), ALU.add
                                ).then_inc(bias_in, 1)
            with pool.Fori(0, NCH) as m:
                rstd(NCH + m)

            def root_h(m, par):
                root(sq_h[:, ds(BC * m, BC)], of_chunk(n_h, par), h_sq_in, n_h_ok, m + 1)

            def root_v(at, par):
                root(of_chunk(v_sq, par), of_chunk(n_v, par), v_sq_in, n_v_ok, at + 1)

            def roots_of_pair(i):
                for par in (0, 1):
                    root_v(2 * i + par, par)
                for par in (0, 1):
                    root(of_chunk(h2_sq, par), of_chunk(n_h2, par), h2_sq_in, n_h2_ok,
                         2 * i + par + 1)

            for m in (0, 1):
                rstd(2 * NCH + m)
                root_h(m, m)
            with pool.Fori(0, NCH // 2 - 1) as i:
                roots_of_pair(i)
                for par in (0, 1):
                    rstd(2 * NCH + 2 * i + 2 + par)
                    root_h(2 * i + 2 + par, par)
            roots_of_pair(NCH // 2 - 1)
            with pool.Fori(0, NCH // 2) as i:
                for par in (0, 1):
                    root(of_chunk(a_sq, par), of_chunk(n_a, par), a_sq_in, n_a_ok,
                         2 * i + par + 1)
                root(cat_sq, n_cat, cat_sq_in, n_cat_ok, i + 1)
                for par in (0, 1):
                    root_v(NCH + 2 * i + par, par)

        @block.scalar
        def _(act):
            a = nc.scalar
            one = lambda v: v.rearrange("(a n) -> a n", a=1).broadcast_to([P, v.shape[0]])
            for dst, src in ((alpha_c, one(alpha)), (beta_c, one(beta)),
                             (kernel_sb[:, :], l1_kernel), (w_sb[:, :], l2_w),
                             (embed_top[:, 0, :], embed), (embed_top[:, 1, :], layer[0:D, :]),
                             (bot_ident[:, 0, :], layer[D:2 * D, :]),
                             (l1_bias_bc, one(l1_bias)), (l2_b_bc, one(l2_b)),
                             (eb_bc, one(embed_bias)), (lb_bc, one(layer_bias))):
                act.dma_start(dst, src).then_inc(params_in, 16)
            act.dma_start(l1b.rearrange("p (c t) -> p c t", t=2),
                          l1_beta.rearrange("(c p t) -> p c t", p=P, t=2)).then_inc(params_in, 16)
            def cast_quarter(i, m, r):
                hh, b = m // BC, m % BC
                if r == 0:
                    act.wait_ge(adj_in[m % 2], (HPC // 2 * i + m // 2 + 1) * 16)
                    act.wait_ge(turned, HPC * i + m + 1)
                cut = slice(HALF // 2 * r, HALF // 2 * (r + 1))
                last = a.activation(bytes8[:, m % 2, cut], stage[:, m % 2, cut], ACT.Copy,
                                    scale=A_BYTE,
                                    accum_out=deg_parts[:, ds(BC * i + b, 1), 2 * hh + r])
                if r:
                    last.then_inc(cast_done, 1)

            def cast_half(i, m):
                for r in range(2):
                    cast_quarter(i, m, r)

            def relu_group(n):
                act.wait_ge(scale_ok, n + 1)
                for k in range(GB * n, GB * (n + 1)):
                    last = a.activation(h0f[:, k // 2, k % 2, :], x[:, k, :], ACT.Relu,
                                        bias=nb0[:, k:k + 1], scale=rs0[:, k:k + 1])
                    if k % BC == BC - 1:
                        last.then_inc(relu_ok, 1)

            def put_ut(q):
                act.wait_ge(ut_ps, q + 1)
                a.activation(u_t[:, :, CW * q:CW * (q + 1)],
                             ps_s16[:, q % 4, :].rearrange("p (r i) -> p r i", r=2), ACT.Copy
                             ).then_inc(ut_ok, 1)

            for n in range(NG):
                relu_group(n)
                cast_half(0, n)
            act.wait_ge(params_in, 16 * N_PARAMS)
            a.activation(e_alpha, alpha_c, ACT.Exp, scale=-1.0).then_inc(sig_e, 1)
            put_ut(0)
            put_ut(1)
            cast_half(0, 4)
            put_ut(2)
            put_ut(3)
            cast_half(0, 5)
            cast_half(0, 6)
            put_ut(4)
            put_ut(5)
            cast_half(0, 7)
            put_ut(6)
            put_ut(7)

            def exp_step(s, base):
                act.wait_ge(z_done, base + s + 1)
                act.wait_ge(elo_done, base + s + 1)
                a.activation(ez[:, s % RING, :], ps_s[:, s % RING, :], ACT.Exp, scale=beta_s,
                             bias=shift_c).then_inc(exp_done, 1)

            act.wait_ge(col_ok, 1)
            with act.Fori(0, NCH - 1) as i:
                for s in range(NB):
                    exp_step(s, NB * i)
                    if s in CAST_AT:
                        m = CAST_AT.index(s)
                        cast_quarter(i + 1, m // 2, m % 2)

            def high_hd(m):
                act.wait_ge(pow_ok, NCH)
                act.wait_ge(hd_sum, m + 1)
                hd = hd_of(m)
                for b in range(BC):
                    a.activation(hd[:, b, :], hd[:, b, :], ACT.Copy,
                                 scale=dis[:, BC * m + b:BC * m + b + 1])
                act.drain()
                a.activation(h_c[:, BC * m:BC * (m + 1), HI, :], hd, ACT.Copy
                             ).then_inc(hd_hi, 1)

            for s in range(NB):
                exp_step(s, NB * (NCH - 1))
                if s in HD_AT:
                    high_hd(HD_AT.index(s))
            for m in range(len(HD_AT), NCH):
                high_hd(m)

            def agg_evac(at, par, bank=None):
                act.wait_ge(agg_done, at + 1)
                act.wait_ge(w_done, at + 1)
                a.activation(agg_sb, ps_acc[:, par, :] if bank is None else bank, ACT.Copy,
                             scale=1.0 / (H_SCALE * A_VALUE)).then_inc(agg_out, 1)

            def relu_chunk(m, at):
                act.wait_ge(l_scale, at + 1)
                act.wait_ge(l_split, at + 1)
                for b in range(BC):
                    last = a.activation(hf[:, b, :], x[:, ds(BC * m + b, 1), :]
                                        .rearrange("p a f -> p (a f)"), ACT.Relu,
                                        bias=nb[:, b:b + 1], scale=rs[:, b:b + 1])
                last.then_inc(l_relu, 1)

            def ht_evac(at):
                act.wait_ge(ht_ps, at + 1)
                a.activation(ht_sb, ps_t[:, 0, :], ACT.Copy, scale=1.0 / H_SCALE
                             ).then_inc(ht_out, 1)

            def layer0_chunk(m, bank):
                agg_evac(m, None, bank)
                relu_chunk(m, m)
                ht_evac(m)

            for m in (0, 1):
                layer0_chunk(m, ps_t[:, m, :])
            with act.Fori(0, NCH // 2 - 1) as i:
                for par in range(2):
                    layer0_chunk(2 * i + 2 + par, ps_acc[:, par, :])
            with act.Fori(0, NCH // 2) as i:
                for par in range(2):
                    agg_evac(NCH + 2 * i + par, par)
                    relu_chunk(2 * i + par, NCH + 2 * i + par)

            def squares(src, dst, scale=1.0, ready=None, count=0):
                act.drain()
                if ready is not None:
                    act.wait_ge(ready, count)
                for b in range(BC):
                    last = a.activation(act_junk[:, b, :], src(b), ACT.Square, scale=scale,
                                        accum_out=dst(b))
                return last

            def squares_h(m):
                squares(lambda b: hf[:, b, :], lambda b: sq_h[:, ds(BC * m + b, 1)],
                        scale=1.0 / H_SCALE).then_inc(h_sq_in, 1)

            def prep_evac(m, par):
                act.wait_ge(prep_done, NCH + m + 1)
                a.activation(v0[:, BC * par:BC * (par + 1), :], prep_out2[:, :, 0, :], ACT.Copy
                             ).then_inc(v_out, 1)
                squares(lambda b: prep_out2[:, b, 0, :],
                        lambda b: v_sq[:, BC * par + b:BC * par + b + 1]).then_inc(v_sq_in, 1)
                a.activation(hw[:, ds(BC * m, BC), :], prep_out2[:, :, 1, :], ACT.Copy
                             ).then_inc(hw_out, 1)

            def ln_step(k):
                act.wait_ge(ln_in, k)
                a.activation(at_l, at_u, ACT.Ln).then_inc(ln_out, 1)

            def tanh_step(k, src):
                act.wait_ge(tanh_in, k)
                a.activation(th, src, ACT.Tanh).then_inc(tanh_out, 1)

            def squares_h2(i):
                for par in range(2):
                    squares(lambda b: g_f[:, BC * par + b, :],
                            lambda b: h2_sq[:, BC * par + b:BC * par + b + 1],
                            ready=h2_ok, count=2 * i + par + 1
                            ).then_inc(h2_sq_in, 1)

            agg_evac(2 * NCH, 0)
            relu_chunk(0, 2 * NCH)
            squares_h(0)
            agg_evac(2 * NCH + 1, 1)
            ht_evac(NCH)
            relu_chunk(1, 2 * NCH + 1)
            squares_h(1)
            prep_evac(0, 0)
            with act.Fori(0, NCH // 2 - 1) as i:
                m = 2 * i + 2
                ht_evac(NCH + m - 1)
                ln_step(2 * i + 1)
                prep_evac(m - 1, 1)
                tanh_step(i + 1, n_v)
                agg_evac(2 * NCH + m, 0)
                squares_h2(i)
                ln_step(2 * i + 2)
                agg_evac(2 * NCH + m + 1, 1)
                relu_chunk(m, 2 * NCH + m)
                squares_h(m)
                ht_evac(NCH + m)
                relu_chunk(m + 1, 2 * NCH + m + 1)
                squares_h(m + 1)
                prep_evac(m, 0)
            i = NCH // 2 - 1
            ht_evac(2 * NCH - 1)
            ln_step(2 * i + 1)
            prep_evac(NCH - 1, 1)
            tanh_step(i + 1, n_v)
            squares_h2(i)
            ln_step(2 * i + 2)

            def layer3_pair(i, banks):
                for par in range(2):
                    agg_evac(3 * NCH + 2 * i + par, par, banks[par])
                    squares(lambda b: w_out2[:, BC * par + b, 1, :],
                            lambda b: a_sq[:, BC * par + b:BC * par + b + 1],
                            ready=w_done, count=3 * NCH + 2 * i + par + 2
                            ).then_inc(a_sq_in, 1)
                tanh_step(NCH // 2 + 2 * i + 1, n_a)
                for par in range(2):
                    squares(lambda b: v0[:, BC * par + b, :],
                            lambda b: v_sq[:, BC * par + b:BC * par + b + 1],
                            ready=v_ok, count=2 * i + par + 1
                            ).then_inc(v_sq_in, 1)
                ln_step(NCH + i + 1)
                tanh_step(NCH // 2 + 2 * i + 2, n_v)

            with act.Fori(0, NCH // 4) as j:
                layer3_pair(2 * j, (ps_acc[:, 0, :], ps_acc[:, 1, :]))
                layer3_pair(2 * j + 1, (ps_t[:, 1, :], ps_t[:, 0, :]))

        @block.vector
        def _(dve):
            v = nc.vector
            def scale0(n):
                g = slice(GB * n, GB * (n + 1))
                dve.wait_ge(rstd_ok, n + 1)
                v.tensor_scalar(rs0[:, g], rs0[:, g], H_SCALE, None, ALU.mult)
                dve.drain()
                v.scalar_tensor_tensor(nb0[:, g], mv0[:, g, 0], -1.0, rs0[:, g], ALU.mult,
                                       ALU.mult).then_inc(scale_ok, 1)

            for n in range(NG):
                dve.wait_ge(x_loaded[n], 16)
                for k in range(GB):
                    v.bn_stats(st[:, k, :], x[:, GB * n + k, :])
                dve.drain()
                for k in range(GB):
                    v.bn_aggr(mv0[:, GB * n + k, :], st[:, k, :])
                dve.drain()
                v.tensor_scalar(rs0[:, GB * n:GB * (n + 1)], mv0[:, GB * n:GB * (n + 1), 1],
                                LN_EPS, None, ALU.add).then_inc(stats_ok, 1)
                if n:
                    scale0(n - 1)
            scale0(NG - 1)

            def high_h(n):
                for q in (2 * n, 2 * n + 1):
                    dve.wait_ge(relu_ok, q + 1)
                    dst = h_a[:, BC * q:BC * (q + 1), :, 0:D].rearrange(
                        "p (c t) r f -> p c t r f", t=2)
                    v.tensor_copy(dst[:, :, :, HI, :], h0f[:, 2 * q:2 * q + 2]
                                  ).then_inc(hi_ok, 1)
                    for b in range(BC):
                        k = BC * q + b
                        h = h0f[:, k // 2, k % 2, :]
                        last = v.scalar_tensor_tensor(g_f[:, k % GB, :], h,
                                                      1.0 / (H_SCALE * H_SCALE), h, ALU.mult,
                                                      ALU.mult, accum_out=sq_h[:, k:k + 1])
                last.then_inc(sq_ok, 1)
                dve.drain()

            run_pairs = run0.rearrange("p (c t) -> p c t", t=2)

            def high_u(n):
                g = slice(GB * n, GB * (n + 1))
                dve.wait_ge(norm_ok, n + 1)
                v.tensor_scalar(run0[:, g], norm0[:, g], COS_EPS, None, ALU.max)
                dve.drain()
                v.reciprocal(run0[:, g], run0[:, g])
                dve.drain()
                v.tensor_scalar(run0[:, g], run0[:, g], U_SCALE / H_SCALE, None, ALU.mult)
                dve.drain()
                quarters = [slice(2 * q, 2 * q + 2) for q in (2 * n, 2 * n + 1)]
                for cs in quarters:
                    v.tensor_tensor(u0f[:, cs], h0f[:, cs], run_pairs[:, cs, :].unsqueeze(3)
                                    .broadcast_to([P, 2, 2, D]), ALU.mult)
                dve.drain()
                for cs in quarters:
                    v.tensor_copy(u0p[:, cs, :, HI, :], u0f[:, cs]).then_inc(u_hi_ok, 1)

            def place(m, col, n):
                hh = m // BC
                dve.wait_ge(turned, n + 3)
                v.tensor_copy(adj_t[:, TPH * hh:TPH * (hh + 1), col],
                              ps_t16[:, m % 2, :].bitcast(U16).rearrange("p (c i) -> p c i", i=P)
                              ).then_inc(adj_placed, 1)

            def place_first(m):
                place(m, slice(P * (m % BC), P * (m % BC + 1)), m)

            def x_minus_h(c, blocks):
                v.scalar_tensor_tensor(pairs(x[:, blocks, :]), h0f[:, c, :, :], x_coef,
                                       pairs(x[:, blocks, :]), ALU.mult, ALU.add)
                dve.drain()

            high_h(0)
            for n in range(1, NG):
                high_h(n)
                high_u(n - 1)
                place_first(n - 1)
            high_u(NG - 1)
            place_first(3)

            dve.wait_ge(params_in, 16 * N_PARAMS)
            dve.wait_ge(sig_e, 1)
            v.tensor_scalar(sig_c, e_alpha, 1.0, None, ALU.add)
            v.tensor_scalar(beta_s, beta_c, 1.0 / (U_SCALE * U_SCALE * A_BYTE), None, ALU.mult)
            v.tensor_scalar(shift_c, beta_c, 0.0, -1.0, ALU.max, ALU.mult)
            dve.drain()
            v.reciprocal(sig_c, sig_c)
            v.tensor_scalar(shift_c, shift_c, E_SHIFT, None, ALU.add).then_inc(col_ok, 1)
            dve.drain()
            v.tensor_scalar(sig_h, sig_c, 1.0 / H_SCALE, None, ALU.mult)
            v.tensor_scalar(x_coef, sig_c, 1.0, -1.0 / H_SCALE, ALU.add, ALU.mult)
            for n, (y, y2) in enumerate(((eb_bc, y2_embed), (lb_bc, y2_layer))):
                v.scalar_tensor_tensor(g_f[:, n, :], y, 1.0, y, ALU.mult, ALU.mult, accum_out=y2)
            dve.drain()
            for m in range(4, HPC):
                place_first(m)

            def z_step(s, base, col, chunk):
                if s % NB == 0:
                    dve.wait_ge(adj_placed, HPC * (chunk + 1) + 2)
                dve.wait_ge(s_done, base + s + 1)
                k = s % NB
                v.tensor_tensor(ps_s[:, s % RING, :], ps_s[:, s % RING, :],
                                adj_u8[:, k // 2, col, k % 2], ALU.mult).then_inc(z_done, 1)

            def high_part(s, base):
                dve.wait_ge(exp_done, base + s + RING + 1)
                dve.wait_ge(e_used, base + s + 1)
                v.tensor_copy(e_parts[:, HI, s % RING, :], ez[:, s % RING, :]
                              ).then_inc(ehi_done, 1)

            def att_tail(i):
                dve.wait_ge(e_used, NB * (i + 1) + RING)
                v.reciprocal(rec, att_acc[:, :, D])
                dve.drain()
                v.tensor_scalar(rec, rec, sig_h, None, ALU.mult)
                dve.drain()
                for b in range(BC):
                    xb = x[:, ds(BC * i + b, 1), :].rearrange("p a f -> p (a f)")
                    last = v.scalar_tensor_tensor(xb, att_acc[:, b, 0:D], rec[:, b:b + 1], xb,
                                                  ALU.mult, ALU.add)
                    if b % 2:
                        last.then_inc(acc_free, 1)

            def degrees(i):
                cut = ds(BC * i, BC)
                dve.wait_ge(adj_placed, HPC * (i + 1) + 2)
                v.tensor_reduce(deg[:, cut], deg_parts[:, cut, :], mybir.AxisListType.X,
                                ALU.add)
                dve.drain()
                v.tensor_scalar(deg[:, cut], deg[:, cut], 1.0 / A_BYTE, None, ALU.mult)
                dve.drain()
                v.tensor_scalar(dis[:, cut], deg[:, cut], 1.0, None, ALU.max
                                ).then_inc(pow_in, 1)

            def sum_hd(m):
                hm = h_a[:, BC * m:BC * m + BC, :, 0:D]
                v.tensor_tensor(hd_of(m), hm[:, :, HI, :], hm[:, :, LO, :], ALU.add
                                ).then_inc(hd_sum, 1)

            def low_hd(m):
                dve.wait_ge(hd_hi, m + 1)
                dst = h_c[:, BC * m:BC * (m + 1), :, :]
                v.tensor_tensor(dst[:, :, LO, :], hd_of(m), dst[:, :, HI, :], ALU.subtract
                                ).then_inc(hd_ok, 1)

            for s in range(Z_AHEAD):
                z_step(s, 0, slice(0, CW), 0)
            for s in range(EARLY):
                z_step(s + Z_AHEAD, 0, slice(0, CW), 0)
                high_part(s, 0)
            x_minus_h(slice(NP - 2, NP), slice(NB - BC, NB))
            with dve.Fori(0, NCH - 1) as i:
                for s in range(EARLY, NB + EARLY):
                    if s in PLACE_AT:
                        m = PLACE_AT.index(s)
                        place(m, ds(CW * (i + 1) + P * (m % BC), P), HPC * (i + 1) + m)
                    z_s = s + Z_AHEAD
                    z_step(z_s, NB * i, ds(CW * (i + z_s // NB), CW), i + z_s // NB)
                    high_part(s, NB * i)
                    if s == 16:
                        degrees(i)
                    if s == EARLY + 2:
                        x_minus_h(ds(2 * i, 2), ds(BC * i, BC))
                att_tail(i)
            for s in range(EARLY, NB):
                if s + Z_AHEAD < NB:
                    z_step(s + Z_AHEAD, NB * (NCH - 1), slice(CW * (NCH - 1), N), NCH - 1)
                high_part(s, NB * (NCH - 1))
                if s == EARLY:
                    degrees(NCH - 1)
                if s + 1 in HD_AT:
                    sum_hd(HD_AT.index(s + 1))
                if s - 3 in HD_AT:
                    low_hd(HD_AT.index(s - 3))
            for m in (4, 5):
                sum_hd(m)
            att_tail(NCH - 1)
            for m in (4, 5, 6, 7):
                low_hd(m)
                if m + 2 < NCH:
                    dve.drain()
                    sum_hd(m + 2)
            v.tensor_scalar(d2, deg, 1.0, None, ALU.add).then_inc(pow_in, 1)
            v.tensor_tensor(inv_deg, deg, l1b, ALU.add)
            dve.drain()
            v.reciprocal(inv_deg, inv_deg)
            dve.drain()
            v.tensor_tensor(inv_beta, inv_deg, l1b, ALU.mult)
            dve.drain()

            def update_x(col, src, m):
                for b in range(BC):
                    xb = x[:, ds(BC * m + b, 1), :].rearrange("p a f -> p (a f)")
                    v.scalar_tensor_tensor(xb, src[:, b, :], col[:, ds(BC * m + b, 1)], xb,
                                           ALU.mult, ALU.add)
                dve.drain()

            def norm_stats(m):
                for b in range(BC):
                    v.bn_stats(st[:, b, :], x[:, ds(BC * m + b, 1), :]
                               .rearrange("p a f -> p (a f)"))
                dve.drain()
                for b in range(BC):
                    v.bn_aggr(mv[:, b, :], st[:, b, :])
                dve.drain()
                v.tensor_scalar(ve, mv[:, :, 1], LN_EPS, None, ALU.add).then_inc(l_stats, 1)

            def norm_scale(L, m):
                dve.wait_ge(l_rstd, NCH * L + m + 1)
                if L == 1:
                    v.scalar_tensor_tensor(rs, ve, H_SCALE, d2[:, ds(BC * m, BC)],
                                           ALU.mult, ALU.mult)
                else:
                    v.tensor_scalar(rs, ve, H_SCALE, None, ALU.mult)
                dve.drain()
                v.scalar_tensor_tensor(nb, mv[:, :, 0], -1.0, rs, ALU.mult, ALU.mult
                                       ).then_inc(l_scale, 1)

            def split(dst, src, done):
                v.tensor_copy(dst[:, :, HI, :], src)
                dve.drain()
                v.tensor_tensor(dst[:, :, LO, :], src, dst[:, :, HI, :], ALU.subtract
                                ).then_inc(done, 1)

            def split_h(L, m):
                dve.wait_ge(l_relu, NCH * L + m + 1)
                split(hs if L == 2 else parts_of(L % 2)[:, ds(BC * m, BC), :, :], hf, l_split)

            dve.wait_ge(pow_ok, NCH + 1)
            with dve.Fori(0, NCH) as m:
                dve.wait_ge(w_done, m + 2)
                update_x(dis, w_out, m)
                norm_stats(m)
                norm_scale(0, m)
                split_h(0, m)
                dve.wait_ge(prep_done, m + 1)
                dve.wait_ge(bias_in, m + 1)
                update_x(inv_beta, prep_out, m)
            with dve.Fori(0, NCH) as m:
                dve.wait_ge(w_done, NCH + m + 2)
                update_x(inv_deg, w_out, m)
                norm_stats(m)
                norm_scale(1, m)
                split_h(1, m)


            def atanh_begin(n, factor):
                v.tensor_scalar(at_n, n, EPS, MAX_TANH, ALU.max, ALU.min)
                v.tensor_scalar(n, n, EPS, None, ALU.max)
                dve.drain()
                v.tensor_scalar(at_o, at_n, -1.0, 1.0, ALU.mult, ALU.add)
                dve.drain()
                v.reciprocal(at_o, at_o)
                dve.drain()
                v.scalar_tensor_tensor(at_t, at_n, 2.0, at_o, ALU.mult, ALU.mult)
                dve.drain()
                v.tensor_scalar(at_u, at_t, 1.0, None, ALU.add).then_inc(ln_in, 1)
                dve.drain()
                v.scalar_tensor_tensor(at_w, at_u, -1.0, n, ALU.add, ALU.mult)
                dve.drain()
                v.reciprocal(at_w, at_w)
                dve.drain()
                v.scalar_tensor_tensor(at_w, at_t, 0.5 * factor, at_w, ALU.mult, ALU.mult)
                dve.drain()

            def atanh_end(dst, k):
                dve.wait_ge(ln_out, k)
                v.tensor_tensor(dst, at_l, at_w, ALU.mult)
                dve.drain()

            def dot_with(y, ready, count):
                for par in range(2):
                    dve.wait_ge(ready, count + par + 1)
                    for b in range(BC * par, BC * (par + 1)):
                        v.scalar_tensor_tensor(tmp[:, b % BC, :], v0[:, b, :], 1.0, y,
                                               ALU.mult, ALU.mult, accum_out=v_y[:, b:b + 1])
                    dve.drain()

            def exp_map_add(scale, y2, at, k_tanh):
                dve.wait_ge(n_v_ok, at + 2)
                v.tensor_tensor(n_v, n_v, scale, ALU.mult)
                dve.drain()
                v.tensor_scalar(n_v, n_v, EPS, None, ALU.max).then_inc(tanh_in, 1)
                dve.drain()
                v.reciprocal(th_q, n_v)
                dve.drain()
                v.tensor_tensor(th_q, th_q, scale, ALU.mult)
                dve.drain()
                v.scalar_tensor_tensor(th_a, v_y, 2.0, th_q, ALU.mult, ALU.mult)
                v.tensor_tensor(th_x, v_sq, th_q, ALU.mult)
                dve.drain()
                v.tensor_tensor(th_x, th_x, th_q, ALU.mult)
                dve.drain()
                dve.wait_ge(tanh_out, k_tanh)
                v.tensor_tensor(th_q, th_q, th, ALU.mult)
                v.tensor_tensor(th_a, th_a, th, ALU.mult)
                v.tensor_tensor(th_x, th_x, th, ALU.mult)
                dve.drain()
                v.tensor_tensor(x2, th_x, th, ALU.mult)
                v.tensor_scalar(a_c, th_a, 1.0, None, ALU.add)
                dve.drain()
                v.scalar_tensor_tensor(b_c, x2, y2, a_c, ALU.mult, ALU.add)
                v.scalar_tensor_tensor(th_q, a_c, y2, th_q, ALU.add, ALU.mult)
                v.tensor_scalar(x2, x2, -1.0, 1.0, ALU.mult, ALU.add)
                dve.drain()
                v.tensor_scalar(b_c, b_c, EPS, None, ALU.max)
                dve.drain()
                v.reciprocal(b_c, b_c)
                dve.drain()
                v.tensor_tensor(a_c, th_q, b_c, ALU.mult)
                v.tensor_tensor(b_c, b_c, x2, ALU.mult)
                dve.drain()

            def layer2_x(m):
                dve.wait_ge(w_done, 2 * NCH + m + 2)
                for b in range(BC):
                    v.scalar_tensor_tensor(tmp[:, b, :], w_out[:, b, :],
                                           d2[:, ds(BC * m + b, 1)], l2_b_bc, ALU.mult, ALU.add)
                dve.drain()
                xc = x[:, ds(BC * m, BC), :]
                v.scalar_tensor_tensor(xc, tmp, 0.0, xc, ALU.max, ALU.add)
                dve.drain()
                norm_stats(m)

            def embed_begin(i):
                dve.wait_ge(n_h_ok, 2 * i + 2)
                atanh_begin(n_h, 1.0)
                atanh_end(l_h, 2 * i + 1)
                dot_with(eb_bc, v_out, 2 * i)
                exp_map_add(l_h, y2_embed, 2 * i, i + 1)
                for b in range(PB):
                    v.tensor_scalar(g_f[:, b, :], eb_bc, b_c[:, b:b + 1], None, ALU.mult)
                dve.drain()
                for b in range(PB):
                    last = v.scalar_tensor_tensor(g_f[:, b, :], v0[:, b, :], a_c[:, b:b + 1],
                                                  g_f[:, b, :], ALU.mult, ALU.add)
                    if b % BC == BC - 1:
                        last.then_inc(h2_ok, 1)

            def log_begin(i):
                dve.wait_ge(n_h2_ok, 2 * i + 2)
                atanh_begin(n_h2, H_SCALE)

            def log_end(i, par):
                cut = slice(BC * par, BC * (par + 1))
                v.tensor_tensor(g_f[:, cut, :], g_f[:, cut, :], l_h[:, cut].unsqueeze(2)
                                .broadcast_to([P, BC, D]), ALU.mult)
                dve.drain()
                split(parts_of(0)[:, ds(BC * (2 * i + par), BC), :, :], g_f[:, cut, :], split_g)

            for m in range(2):
                layer2_x(m)
                norm_scale(2, m)
                split_h(2, m)
            with dve.Fori(0, NCH // 2 - 1) as i:
                m = 2 * i + 2
                embed_begin(i)
                layer2_x(m)
                log_begin(i)
                norm_scale(2, m)
                atanh_end(l_h, 2 * i + 2)
                split_h(2, m)
                layer2_x(m + 1)
                log_end(i, 0)
                norm_scale(2, m + 1)
                log_end(i, 1)
                split_h(2, m + 1)
            embed_begin(NCH // 2 - 1)
            log_begin(NCH // 2 - 1)
            atanh_end(l_h, NCH)
            log_end(NCH // 2 - 1, 0)
            log_end(NCH // 2 - 1, 1)

            with dve.Fori(0, NCH // 2) as i:
                dve.wait_ge(n_a_ok, 2 * i + 2)
                v.tensor_scalar(n_a, n_a, EPS, None, ALU.max).then_inc(tanh_in, 1)
                dve.drain()
                v.reciprocal(r_a, n_a)
                dve.drain()
                v.tensor_tensor(cat_sq, r_a, r_a, ALU.mult)
                dve.drain()
                v.tensor_tensor(cat_sq, cat_sq, a_sq, ALU.mult)
                dve.drain()
                dve.wait_ge(tanh_out, NCH // 2 + 2 * i + 1)
                v.tensor_tensor(tq, th, r_a, ALU.mult)
                v.tensor_tensor(cat_sq, cat_sq, th, ALU.mult)
                dve.drain()
                v.tensor_tensor(cat_sq, cat_sq, th, ALU.mult)
                dve.drain()
                v.tensor_tensor(cat_sq, cat_sq, sq_h[:, ds(PB * i, PB)], ALU.add
                                ).then_inc(cat_sq_in, 1)
                for b in range(PB):
                    last = v.scalar_tensor_tensor(v0[:, b, :], w_out2[:, b, 0, :], tq[:, b:b + 1],
                                                  hw[:, ds(PB * i + b, 1), :]
                                                  .rearrange("p a f -> p (a f)"),
                                                  ALU.mult, ALU.add)
                    if b % BC == BC - 1:
                        last.then_inc(v_ok, 1)
                dve.drain()
                dve.wait_ge(n_cat_ok, i + 1)
                atanh_begin(n_cat, 1.0)
                dot_with(lb_bc, v_ok, 2 * i)
                atanh_end(l_h, NCH + i + 1)
                exp_map_add(l_h, y2_layer, NCH + 2 * i, NCH // 2 + 2 * i + 2)
                for par in range(2):
                    for b in range(BC * par, BC * (par + 1)):
                        xb = x[:, ds(PB * i + b, 1), :].rearrange("p a f -> p (a f)")
                        v.scalar_tensor_tensor(xb, lb_bc, b_c[:, b:b + 1], xb, ALU.mult, ALU.add)
                    dve.drain()
                    for b in range(BC * par, BC * (par + 1)):
                        xb = x[:, ds(PB * i + b, 1), :].rearrange("p a f -> p (a f)")
                        last = v.scalar_tensor_tensor(xb, v0[:, b, :], a_c[:, b:b + 1], xb,
                                                      ALU.mult, ALU.add)
                    last.then_inc(x_done, 1)

        @block.tensor
        def _(pe):
            t = nc.tensor
            pe.wait_ge(ident_ok, 10)

            def turn(m, half_no):
                pe.wait_ge(cast_done, half_no + 3)
                pe.wait_ge(adj_placed, half_no + 1)
                src = bytes8[:, m % 2, :].bitcast(F16)
                for c in range(TPH):
                    last = t.transpose(ps_t16[:, m % 2, P * c:P * (c + 1)],
                                       src[:, P * c:P * (c + 1)], ident16[:, :])
                last.then_inc(turned, 1)

            def turn_u(q):
                pe.wait_ge(u_ok, q + 1)
                if q >= 4:
                    pe.wait_ge(ut_ok, q - 3)
                dst = ps_s16[:, q % 4, :].rearrange("p (r i) -> p r i", r=2)
                for k in range(BC * q, BC * (q + 1)):
                    for r in (LO, HI):
                        last = t.transpose(dst[:, r, P * (k % BC):P * (k % BC + 1)],
                                           u0p[:, k // 2, k % 2, r, :], ident16[:, :])
                last.then_inc(ut_ps, 1)

            turn(0, 0)
            turn(1, 1)
            turn_u(0)
            turn_u(1)
            turn(2, 2)
            turn_u(2)
            turn_u(3)
            turn(3, 3)
            turn(4, 4)
            turn_u(4)
            turn_u(5)
            turn(5, 5)
            turn_u(6)
            turn_u(7)
            turn(6, 6)
            turn(7, 7)
            pe.wait_ge(ut_ok, NCH)

            def scores(s, base, col):
                pe.wait_ge(exp_done, base + s + 1)
                k = s % NB
                for n, (rj, ri) in enumerate(((HI, HI), (HI, LO), (LO, HI))):
                    last = t.matmul(ps_s[:, s % RING, :], u_t[:, rj, P * k:P * (k + 1)],
                                    u_t[:, ri, col], start=(n == 0), stop=(n == 2))
                last.then_inc(s_done, 1)

            def att_products(s, base, i):
                pe.wait_ge(elo_done, base + s + RING + 1)
                for b in range(BC):
                    if s == 0 and b % 2 == 0:
                        pe.wait_ge(acc_free, 2 * i + b // 2 + 1)
                    for n, (re, rh) in enumerate(((HI, HI), (HI, LO), (LO, HI))):
                        last = t.matmul(att_acc[:, b, 0:D + 1],
                                        e_parts[:, re, s % RING, P * b:P * (b + 1)],
                                        h_a[:, s, rh, 0:D + 1],
                                        start=(s == 0 and n == 0 and b % 2 == 0),
                                        stop=(s == NB - 1 and n == 2),
                                        skip_group_check=True)
                return last

            pe.wait_ge(split0_ok, NCH)
            for s in range(RING):
                scores(s, 0, slice(0, CW))
            with pe.Fori(0, NCH - 1) as i:
                for s in range(NB):
                    if s in TURN_AT:
                        m = TURN_AT.index(s)
                        turn(m, HPC * (i + 1) + m)
                    s_s = s + RING
                    scores(s_s, NB * i, ds(CW * (i + s_s // NB), CW))
                    att_products(s, NB * i, i).then_inc(e_used, 1)
            def aggregate(L, c, q):
                h = parts_of((L + 1) % 2)
                if L == 0 and c < 2:
                    acc = ps_t[:, c, :]
                elif L == 3 and c % 4 >= 2:
                    acc = ps_t[:, 3 - c % 4, :]
                else:
                    acc = ps_acc[:, c % 2, :]
                if q == 0:
                    if L == 3 and c >= 2:
                        if c >= 4:
                            pe.wait_ge(agg_out, NCH * L + c - 3)
                        elif c == 3:
                            pe.wait_ge(ht_out, 2 * NCH)
                    elif L == 0 and c < 2:
                        pe.wait_ge(adj_placed, HPC * NCH + 2)
                    elif L == 0 and c < 4:
                        pe.wait_ge(acc_free, 2 * NCH + c - 1)
                    else:
                        pe.wait_ge(agg_out, NCH * L + c - 1)
                if c < (4 if L == 3 else 2):
                    ready, n = ((hd_ok, 0), (l_split, 1), (l_split, NCH + 1), (split_g, 0))[L]
                    pe.wait_ge(ready, n + q + 1)
                if L == 2 and q == NB // BC - 1:
                    for b in range(BC):
                        for r in (LO, HI):
                            t.matmul(acc[:, P * b:P * (b + 1)], h[:, BC * c + b, r, :],
                                     ident16x2[:, :], start=False, stop=False,
                                     skip_group_check=True)
                for k in range(BC * q, BC * (q + 1)):
                    for r in (LO, HI):
                        last = t.matmul(acc, h[:, k, r, :],
                                        adj_f8[:, k // 2, CW * c:CW * (c + 1), k % 2],
                                        start=(k == 0 and r == LO),
                                        stop=(k == NB - 1 and r == HI))
                if q == NB // BC - 1:
                    last.then_inc(agg_done, 1)

            base = NB * (NCH - 1)
            for s in range(NB):
                if s + RING < NB:
                    scores(s + RING, base, slice(CW * (NCH - 1), N))
                att_products(s, base, NCH - 1).then_inc(e_used, 1)
                if s in FILL_AT:
                    aggregate(0, *QUARTERS_0[FILL_AT.index(s)])

            pe.wait_ge(params_in, 16 * N_PARAMS)


            def weights(L, m):
                at = NCH * L + m
                pe.wait_ge(agg_out, at + 1)
                if L < 3:
                    if at:
                        pe.wait_ge(l_stats, at)
                    rhs = (ident32, kernel_sb[:, :], w_sb[:, :])[L]
                    for b in range(BC):
                        last = t.matmul(w_out[:, b, :], agg_sb[:, P * b:P * (b + 1)], rhs,
                                        start=True, stop=True)
                else:
                    if m == 0:
                        pe.wait_ge(l_stats, 3 * NCH)
                    elif m == 1:
                        pe.wait_ge(hw_out, NCH)
                    else:
                        pe.wait_ge(v_ok, m - 1)
                    for b in range(BC):
                        last = t.matmul(w_out2[:, BC * (m % 2) + b, :, :],
                                        agg_sb[:, P * b:P * (b + 1)],
                                        bot_ident[:, :, :], start=True, stop=True)
                last.then_inc(w_done, 1)

            def turn_h(L, m):
                pe.wait_ge(l_split, NCH * L + m + 2)
                for b in range(BC):
                    for r in (LO, HI):
                        src = hs[:, b, r, :] if L == 2 else parts_of(0)[:, BC * m + b, r, :]
                        last = t.matmul(ps_t[:, 0, P * b:P * (b + 1)], src, ident16[:, :],
                                        start=(r == LO), stop=(r == HI))
                last.then_inc(ht_ps, 1)

            def prepare(L, m):
                pe.wait_ge(ht_out, NCH * (L // 2) + m + 1)
                for b in range(BC):
                    if L == 0:
                        last = t.matmul(prep_out[:, b, :], ht_sb[:, P * b:P * (b + 1)],
                                        kernel_sb[:, :], start=True, stop=True)
                    else:
                        last = t.matmul(prep_out2[:, b, :, :], ht_sb[:, P * b:P * (b + 1)],
                                        embed_top[:, :, :], start=True, stop=True)
                last.then_inc(prep_done, 1)

            def small_steps(L, idx):
                for steps, after in ((weights, W_AFTER), (turn_h, T_AFTER), (prepare, V_AFTER)):
                    for m, at in enumerate(after[L]):
                        if at == idx:
                            steps(L, m)

            for L in range(4):
                quarters = (QUARTERS_0, QUARTERS, QUARTERS, QUARTERS_3)[L]
                for idx, (c, q) in enumerate(quarters):
                    if L or idx >= len(FILL_AT):
                        aggregate(L, c, q)
                    if L:
                        small_steps(L - 1, idx + len(quarters))
                    small_steps(L, idx)
            weights(3, NCH - 1)


_INS = ["x", "adj", "L0_gnn_alpha", "L0_gnn_beta", "L1_gnn_kernel", "L1_gnn_bias", "L1_gnn_beta",
        "L2_gnn_W", "L2_gnn_b", "L3_gnn_embed", "L3_gnn_layer", "L3_gnn_embed_bias",
        "L3_gnn_layer_bias"]


def kernel(**inputs):
    import numpy as np
    import concourse.bacc as bacc
    from concourse.bass_utils import run_bass_kernel_spmd

    nc = bacc.Bacc("TRN2", target_bir_lowering=False, num_devices=1, dynamic_dma_scratch_size=1024)
    arrays, args = {}, []
    for n in _INS:
        v = np.ascontiguousarray(inputs[n])
        v = v.reshape(v.shape or (1,))
        arrays[f"in_{n}"] = v
        args.append(nc.dram_tensor(f"in_{n}", v.shape, mybir.dt.from_np(v.dtype),
                                   kind="ExternalInput").ap())
    out = nc.dram_tensor("out_0", (N, D), F32, kind="ExternalOutput").ap()
    program(nc, *args, out)
    r = run_bass_kernel_spmd(nc, [arrays], core_ids=[0])
    return r.results[0]["out_0"]
```

```python
from contextlib import ExitStack

import concourse.bass as bass
from concourse import mybir

F32, F16 = mybir.dt.float32, mybir.dt.float16
U8, U16, F8 = mybir.dt.uint8, mybir.dt.uint16, mybir.dt.float8e4
ALU, ACT = mybir.AluOpType, mybir.ActivationFunctionType

N, D = 4096, 128
P = 128
NB = N // P
NP = NB // 2
BC = 4
NCH = NB // BC
CW = BC * P
HALF = N // 2
HPC = 2 * BC
TPH = HALF // 2 // P
NG = 4
GB = NB // NG
RING = 4
Z_AHEAD = 1

EARLY = 2

CAST_AT = [3 * m + r for m in range(HPC) for r in (1, 2)]
TURN_AT = [3 * m + 2 for m in range(HPC)]
PLACE_AT = [3 * m + 8 for m in range(HPC)]

HD_AT = [8 + 6 * m for m in range(4)]
FILL_AT = [27, 28, 29, 30]

H_SCALE = 4096.0
U_SCALE = 16384.0
A_BYTE = 64.0
A_VALUE = 2.0
E_SHIFT = 10.0
LN_EPS, COS_EPS, EPS = 1e-5, 1e-8, 1e-7
MAX_TANH = 1.0 - 1e-6

QUARTERS = ([(0, q) for q in range(7)] + [(1, q) for q in range(7)] + [(0, 7), (1, 7)]
            + [(c, q) for c in range(2, NCH) for q in range(8)])
QUARTERS_0 = ([(c, q) for q4 in ((0, 1, 2, 3), (4, 5), (6, 7)) for c in (0, 1) for q in q4]
              + [(c, q) for c in range(2, NCH) for q in range(8)])
QUARTERS_3 = ([(c, q) for q4 in ((0, 1, 2, 3), (4, 5)) for c in (0, 1, 2) for q in q4]
              + [(3, q) for q in range(4)] + [(c, q) for c in (0, 1, 2) for q in (6, 7)]
              + [(3, q) for q in range(4, 8)]
              + [(c, q) for c in range(4, NCH) for q in range(8)])
W_0 = [15, 22, 29, 36, 43, 50, 57, 64]
W_1 = [15, 21, 27, 33, 40, 48, 56, 64]
W_AFTER = (W_0, W_1, [15, 20, 29, 35, 46, 51, 61, 67], [24, 26, 33, 35, 43, 49, 57, 64])
T_AFTER = ([w + 6 for w in W_0], (), [20, 25, 36, 41, 52, 57, 68, 73], ())
V_AFTER = tuple([t + 1 for t in ts] for ts in T_AFTER)


def program(nc, x_in, adj, alpha, beta, l1_kernel, l1_bias, l1_beta, l2_w, l2_b, embed, layer,
            embed_bias, layer_bias, out):
    ctx = ExitStack()
    with ctx:
        def sb(name, shape, dt=F32):
            return ctx.enter_context(nc.sbuf_tensor(name, shape, dt))

        def sem(name):
            return ctx.enter_context(nc.semaphore(name))

        ds = bass.ds

        adj_t = sb("adj_t", [P, NP, N], U16)
        adj_u8 = adj_t[:, :, :].bitcast(U8).rearrange("p c (i t) -> p c i t", t=2)
        adj_f8 = adj_t[:, :, :].bitcast(F8).rearrange("p c (i t) -> p c i t", t=2)
        x = sb("x", [P, NB, D])
        LO, HI = 0, 1
        h_a = sb("h_a", [P, NB, 2, D + 2], F16)
        stage = sb("stage", [P, 2, HALF])
        h_c = stage[:, :, :].rearrange("p a n -> p (a n)").bitcast(F16).rearrange(
            "p (k r f) -> p k r f", r=2, f=D)
        u_t = sb("u_t", [P, 2, N], F16)
        hw = u_t[:, :, :].rearrange("p a n -> p (a n)").bitcast(F32).rearrange(
            "p (k f) -> p k f", f=D)
        bytes8 = sb("bytes8", [P, 2, HALF], U8)
        hd_f = bytes8[:, :, :].bitcast(F32)
        ez = sb("ez", [P, RING, CW])
        e_parts = sb("e_parts", [P, 2, RING, CW], F16)
        agg_sb = ez[:, 0, :]
        hf = ez[:, 1, :].rearrange("p (b f) -> p b f", f=D)
        g_f = ez[:, 2:4, :].rearrange("p a (b f) -> p (a b) f", f=D)
        ep = e_parts[:, :, :, :].rearrange("p a r n -> p (a r n)")
        hs = ep[:, 0:2 * CW].rearrange("p (b r f) -> p b r f", r=2, f=D)
        v0 = ep[:, 2 * CW:6 * CW].bitcast(F32).rearrange("p (b f) -> p b f", f=D)
        act_junk = ep[:, 6 * CW:8 * CW].bitcast(F32).rearrange("p (b f) -> p b f", f=D)
        tmp = bytes8[:, 0, :].bitcast(F32).rearrange("p (b f) -> p b f", f=D)
        ht_sb = bytes8[:, 1, :].bitcast(F32)
        h0f = adj_t[:, :, (NCH - 1) * CW:].bitcast(F32).rearrange("p c (t f) -> p c t f", t=2)
        u0f = adj_t[:, :, 5 * CW:6 * CW].bitcast(F32).rearrange("p c (t f) -> p c t f", t=2)
        u0p = adj_t[:, :, 6 * CW:7 * CW].bitcast(F16).rearrange("p c (t r f) -> p c t r f", r=2,
                                                                t=2)

        kernel_sb = sb("kernel_sb", [D, D])
        w_sb = sb("w_sb", [D, D])
        embed_top = sb("embed_top", [D, 2, D])
        layer_bot_sb = sb("layer_bot_sb", [D, D])
        layer_bot = layer_bot_sb[:, :]
        ident32_sb = sb("ident32_sb", [P, P])
        ident32 = ident32_sb[:, :]
        ident16 = sb("ident16", [P, P], F16)
        ident16x2 = sb("ident16x2", [P, P], F16)
        bias_bc = sb("bias_bc", [P, 4, D])
        l1_bias_bc, l2_b_bc, eb_bc, lb_bc = (bias_bc[:, n, :] for n in range(4))
        scal = sb("scal", [P, 12])
        (alpha_c, beta_c, e_alpha, sig_c, sig_h, x_coef, beta_s, shift_c, y2_embed, y2_layer,
         neg_half, half) = (scal[:, n:n + 1] for n in range(12))
        deg_parts = sb("deg_parts", [P, NB, 4])
        cols = sb("cols", [P, 11, NB])
        (deg, dis, inv_deg, inv_beta, d2, l1b, rs0, nb0, sq_h, norm0, run0) = (
            cols[:, n, :] for n in range(11))
        st = sb("st", [P, GB, 6])
        mv = sb("mv", [P, BC, 2])
        mv0 = sb("mv0", [P, NB, 2])
        small = sb("small", [P, 4, BC])
        rec, ve, rs, nb = (small[:, n, :] for n in range(4))
        PB = 2 * BC
        hyp = sb("hyp", [P, 26, PB])
        (n_h, l_h, v_sq, n_v, v_y, a_c, b_c, at_n, at_o, at_t, at_u, at_l, at_w, th_q, th,
         th_a, th_x, x2, a_sq, n_a, n_h2, cat_sq, n_cat, tq, h2_sq, r_a) = (
            hyp[:, n, :] for n in range(26))

        ps_s = ctx.enter_context(nc.psum_tensor("ps_s", [P, 4, CW], F32))
        ps_acc = ctx.enter_context(nc.psum_tensor("ps_acc", [P, 2, CW], F32))
        ps_t = ctx.enter_context(nc.psum_tensor("ps_t", [P, 2, CW], F32))
        ps_t16 = ps_t[:, :, :].bitcast(F16)
        ps_s16 = ps_s[:, :, :].bitcast(F16)
        att_acc = ps_acc[:, :, :].rearrange("p k (b f) -> p (k b) f", b=2)
        w_out = ps_s[:, 0, :].rearrange("p (b f) -> p b f", f=D)
        w_out2 = ps_s[:, :, :].rearrange("p (a r) (b f) -> p a r b f", r=2, f=D)
        prep_out = ps_s[:, 2, :].rearrange("p (b f) -> p b f", f=D)
        prep_out2 = ps_s[:, 2:4, :].rearrange("p a (b r f) -> p (a b) r f", b=2, r=2)

        names = ("params_in stored cast_done turned adj_placed ident_ok sig_e col_ok stats_ok "
                 "rstd_ok scale_ok relu_ok hi_ok sq_ok norm_ok split0_ok u_hi_ok u_ok ut_ps "
                 "ut_ok ut_last_ok s_done z_done exp_done ehi_done elo_done e_used acc_free "
                 "pow_in pow_ok hd_sum hd_hi hd_ok agg_done agg_out agg_turned w_done l_stats "
                 "l_rstd l_scale l_relu l_split ht_ps ht_out prep_done bias_in hw_out x_done "
                 "h_sq_in n_h_ok v_sq_in n_v_ok h2_sq_in n_h2_ok a_sq_in n_a_ok cat_sq_in "
                 "n_cat_ok tanh_in tanh_out ln_in ln_out h2_ok v_ok v_out split_g").split()
        adj_in = [sem("adj_in0"), sem("adj_in1")]
        x_loaded = [sem(f"x_loaded{n}") for n in range(NG)]
        (params_in, stored, cast_done, turned, adj_placed, ident_ok, sig_e, col_ok, stats_ok,
         rstd_ok, scale_ok, relu_ok, hi_ok, sq_ok, norm_ok, split0_ok, u_hi_ok, u_ok, ut_ps,
         ut_ok, ut_last_ok, s_done, z_done, exp_done, ehi_done, elo_done, e_used, acc_free,
         pow_in, pow_ok, hd_sum, hd_hi, hd_ok, agg_done, agg_out, agg_turned, w_done, l_stats,
         l_rstd, l_scale, l_relu, l_split, ht_ps, ht_out, prep_done, bias_in, hw_out, x_done,
         h_sq_in, n_h_ok, v_sq_in, n_v_ok, h2_sq_in, n_h2_ok, a_sq_in, n_a_ok, cat_sq_in,
         n_cat_ok, tanh_in, tanh_out, ln_in, ln_out, h2_ok, v_ok, v_out, split_g) = (
            sem(n) for n in names)

        adj_rows = adj.rearrange("(c p t) n -> p c t n", p=P, t=2)
        x_view = x_in.rearrange("(c p t) f -> p c t f", p=P, t=2)
        out_view = out.rearrange("(c p t) f -> p c t f", p=P, t=2)
        N_PARAMS = 12

        def parts_of(buf):
            return h_c if buf else h_a[:, :, :, 0:D]

        PAIR = slice(0, PB)

        def part_cut(pars):
            return slice(BC * pars[0], BC * (pars[-1] + 1))

        def hd_of(m):
            return hd_f[:, m % 2, :].rearrange("p (b f) -> p b f", f=D)

        def pairs(ap):
            return ap.rearrange("p (c t) f -> p c t f", t=2)

        block = ctx.enter_context(nc.Block())

        @block.sync
        def _(sp):
            for s, n in ((cast_done, 2), (turned, 2), (adj_placed, 2), (exp_done, RING),
                         (elo_done, RING), (e_used, RING), (acc_free, 2), (w_done, 1),
                         (l_split, 1)):
                sp.sem_inc(s, n)
            for n in range(NG):
                sp.dma_start(x[:, GB * n:GB * (n + 1), :].rearrange("p (c t) f -> p c t f", t=2),
                             x_view[:, GB // 2 * n:GB // 2 * (n + 1), :, :]
                             ).then_inc(x_loaded[n], 16)
            with sp.Fori(0, NCH) as i:
                for m in range(HPC):
                    hh, b = m // BC, m % BC
                    sp.wait_ge(cast_done, HPC * i + m + 1)
                    sp.dma_start(stage[:, m % 2, :],
                                 adj_rows[:, ds(2 * i + b // 2, 1), b % 2,
                                          hh * HALF:(hh + 1) * HALF]
                                 .rearrange("p a n -> p (a n)")).then_inc(adj_in[m % 2], 16)
            with sp.Fori(0, NCH) as m:
                sp.wait_ge(x_done, m + 1)
                sp.dma_start(out_view[:, ds(2 * m, 2), :, :], pairs(x[:, ds(BC * m, BC), :])
                             ).then_inc(stored, 16)
            sp.wait_ge(stored, 16 * NCH)

        @block.gpsimd
        def _(pool):
            g = nc.gpsimd
            g.memset(ident16[:, :], 0.0).then_inc(ident_ok, 1)
            g.memset(ident16x2[:, :], 0.0).then_inc(ident_ok, 1)
            g.memset(ident32, 0.0).then_inc(ident_ok, 1)
            pool.wait_ge(ident_ok, 3)
            for m, v in ((ident16[:, :], 1.0), (ident16x2[:, :], A_VALUE), (ident32, 1.0)):
                g.affine_select(out=m, in_=m, compare_op=ALU.not_equal, fill=v, base=0,
                                pattern=[[-1, P]], channel_multiplier=1).then_inc(ident_ok, 1)
            g.memset(neg_half, -0.5).then_inc(ident_ok, 1)
            g.memset(half, 0.5).then_inc(ident_ok, 1)
            g.memset(h_a[:, :, LO, D:D + 2], 0.0).then_inc(ident_ok, 1)
            g.memset(h_a[:, :, HI, D:D + 2], 1.0).then_inc(ident_ok, 1)
            pool.wait_ge(ident_ok, 10)

            def power(col, e):
                return g.tensor_tensor(col, col, e.broadcast_to(col.shape), ALU.pow)

            for n in range(NG):
                pool.wait_ge(stats_ok, n + 1)
                power(rs0[:, GB * n:GB * (n + 1)], neg_half).then_inc(rstd_ok, 1)

            def quarter(buf, q):
                return buf[:, 2 * q:2 * q + 2]

            def low_u(q):
                pool.wait_ge(u_hi_ok, q + 1)
                g.tensor_tensor(quarter(u0p, q)[:, :, :, LO, :], quarter(u0f, q),
                                quarter(u0p, q)[:, :, :, HI, :], ALU.subtract).then_inc(u_ok, 1)

            def low_h(q):
                pool.wait_ge(hi_ok, q + 1)
                dst = h_a[:, BC * q:BC * (q + 1), :, 0:D].rearrange(
                    "p (c t) r f -> p c t r f", t=2)
                g.tensor_tensor(dst[:, :, :, LO, :], quarter(h0f, q), dst[:, :, :, HI, :],
                                ALU.subtract).then_inc(split0_ok, 1)

            for n in range(NG):
                cols_n = slice(GB * n, GB * (n + 1))
                pool.wait_ge(sq_ok, n + 1)
                g.tensor_tensor(norm0[:, cols_n], sq_h[:, cols_n], half.broadcast_to([P, GB]),
                                ALU.pow).then_inc(norm_ok, 1)
                if n:
                    low_u(2 * n - 2)
                    low_u(2 * n - 1)
                if n < NG // 2:
                    low_h(2 * n)
                    low_h(2 * n + 1)
            low_u(NCH - 2)
            low_u(NCH - 1)
            for q in range(NCH // 2, NCH):
                low_h(q)

            def low_part(s, base):
                pool.wait_ge(ehi_done, base + s + 1)
                g.tensor_tensor(e_parts[:, LO, s % RING, :], ez[:, s % RING, :],
                                e_parts[:, HI, s % RING, :], ALU.subtract).then_inc(elo_done, 1)

            def root_degree(i):
                pool.wait_ge(pow_in, i + 1)
                power(dis[:, ds(BC * i, BC)], neg_half).then_inc(pow_ok, 1)

            with pool.Fori(0, NCH - 1) as i:
                for s in range(NB):
                    low_part(s, NB * i)
                    if s == 20:
                        root_degree(i)
            for s in range(NB):
                low_part(s, NB * (NCH - 1))
                if s == 6:
                    root_degree(NCH - 1)
            pool.wait_ge(pow_in, NCH + 1)
            power(d2, neg_half).then_inc(pow_ok, 1)

            def rstd(at):
                pool.wait_ge(l_stats, at + 1)
                power(ve, neg_half).then_inc(l_rstd, 1)

            def root(src, dst, ready, done, count):
                pool.wait_ge(ready, count)
                g.tensor_tensor(dst, src, half.broadcast_to(dst.shape), ALU.pow).then_inc(done, 1)

            def of_chunk(cols, par):
                return cols[:, BC * par:BC * (par + 1)]

            with pool.Fori(0, NCH) as m:
                rstd(m)
                pool.wait_ge(l_relu, m + 1)
                g.tensor_tensor(x[:, ds(BC * m, BC), :], x[:, ds(BC * m, BC), :],
                                l1_bias_bc.unsqueeze(1).broadcast_to([P, BC, D]), ALU.add
                                ).then_inc(bias_in, 1)
            with pool.Fori(0, NCH) as m:
                rstd(NCH + m)

            def root_h(m, par):
                root(sq_h[:, ds(BC * m, BC)], of_chunk(n_h, par), h_sq_in, n_h_ok, m + 1)

            def root_v(at, par):
                root(of_chunk(v_sq, par), of_chunk(n_v, par), v_sq_in, n_v_ok, at + 1)

            def roots_of_pair(i):
                for par in (0, 1):
                    root_v(2 * i + par, par)
                for par in (0, 1):
                    root(of_chunk(h2_sq, par), of_chunk(n_h2, par), h2_sq_in, n_h2_ok,
                         2 * i + par + 1)

            for m in (0, 1):
                rstd(2 * NCH + m)
                root_h(m, m)
            with pool.Fori(0, NCH // 2 - 1) as i:
                roots_of_pair(i)
                for par in (0, 1):
                    rstd(2 * NCH + 2 * i + 2 + par)
                    root_h(2 * i + 2 + par, par)
            roots_of_pair(NCH // 2 - 1)
            def roots_of_part(i, pars, k):
                for par in pars:
                    root(of_chunk(a_sq, par), of_chunk(n_a, par), a_sq_in, n_a_ok,
                         2 * i + par + 1)
                cut = part_cut(pars)
                root(cat_sq[:, cut], n_cat[:, cut], cat_sq_in, n_cat_ok, k + 1)
                for par in pars:
                    root_v(NCH + 2 * i + par, par)

            with pool.Fori(0, NCH // 2 - 1) as i:
                roots_of_part(i, (0, 1), i)
            roots_of_part(NCH // 2 - 1, (0,), NCH // 2 - 1)
            roots_of_part(NCH // 2 - 1, (1,), NCH // 2)

        @block.scalar
        def _(act):
            a = nc.scalar
            one = lambda v: v.rearrange("(a n) -> a n", a=1).broadcast_to([P, v.shape[0]])
            for dst, src in ((alpha_c, one(alpha)), (beta_c, one(beta)),
                             (kernel_sb[:, :], l1_kernel), (w_sb[:, :], l2_w),
                             (embed_top[:, 0, :], embed), (embed_top[:, 1, :], layer[0:D, :]),
                             (layer_bot, layer[D:2 * D, :]),
                             (l1_bias_bc, one(l1_bias)), (l2_b_bc, one(l2_b)),
                             (eb_bc, one(embed_bias)), (lb_bc, one(layer_bias))):
                act.dma_start(dst, src).then_inc(params_in, 16)
            act.dma_start(l1b.rearrange("p (c t) -> p c t", t=2),
                          l1_beta.rearrange("(c p t) -> p c t", p=P, t=2)).then_inc(params_in, 16)
            def cast_quarter(i, m, r):
                hh, b = m // BC, m % BC
                if r == 0:
                    act.wait_ge(adj_in[m % 2], (HPC // 2 * i + m // 2 + 1) * 16)
                    act.wait_ge(turned, HPC * i + m + 1)
                cut = slice(HALF // 2 * r, HALF // 2 * (r + 1))
                last = a.activation(bytes8[:, m % 2, cut], stage[:, m % 2, cut], ACT.Copy,
                                    scale=A_BYTE,
                                    accum_out=deg_parts[:, ds(BC * i + b, 1), 2 * hh + r])
                if r:
                    last.then_inc(cast_done, 1)

            def cast_half(i, m):
                for r in range(2):
                    cast_quarter(i, m, r)

            def relu_group(n):
                act.wait_ge(scale_ok, n + 1)
                for k in range(GB * n, GB * (n + 1)):
                    last = a.activation(h0f[:, k // 2, k % 2, :], x[:, k, :], ACT.Relu,
                                        bias=nb0[:, k:k + 1], scale=rs0[:, k:k + 1])
                    if k % BC == BC - 1:
                        last.then_inc(relu_ok, 1)

            def put_ut(q):
                act.wait_ge(ut_ps, q + 1)
                a.activation(u_t[:, :, CW * q:CW * (q + 1)],
                             ps_s16[:, q % 4, :].rearrange("p (r i) -> p r i", r=2), ACT.Copy
                             ).then_inc(ut_ok, 1)

            for n in range(NG):
                relu_group(n)
                cast_half(0, n)
            act.wait_ge(params_in, 16 * N_PARAMS)
            a.activation(e_alpha, alpha_c, ACT.Exp, scale=-1.0).then_inc(sig_e, 1)
            cast_half(0, 4)
            put_ut(0)
            put_ut(1)
            cast_half(0, 5)
            put_ut(2)
            put_ut(3)
            cast_half(0, 6)
            put_ut(4)
            cast_half(0, 7)
            put_ut(5)

            def exp_step(s, base):
                act.wait_ge(z_done, base + s + 1)
                act.wait_ge(elo_done, base + s + 1)
                a.activation(ez[:, s % RING, :], ps_s[:, s % RING, :], ACT.Exp, scale=beta_s,
                             bias=shift_c).then_inc(exp_done, 1)

            act.wait_ge(col_ok, 1)
            with act.Fori(0, NCH - 1) as i:
                for s in range(NB):
                    exp_step(s, NB * i)
                    if s in CAST_AT:
                        m = CAST_AT.index(s)
                        cast_quarter(i + 1, m // 2, m % 2)

            def high_hd(m):
                act.wait_ge(pow_ok, NCH)
                act.wait_ge(hd_sum, m + 1)
                hd = hd_of(m)
                for b in range(BC):
                    a.activation(hd[:, b, :], hd[:, b, :], ACT.Copy,
                                 scale=dis[:, BC * m + b:BC * m + b + 1])
                act.drain()
                a.activation(h_c[:, BC * m:BC * (m + 1), HI, :], hd, ACT.Copy
                             ).then_inc(hd_hi, 1)

            for s in range(NB):
                exp_step(s, NB * (NCH - 1))
                if s in HD_AT:
                    high_hd(HD_AT.index(s))
            for m in range(len(HD_AT), NCH):
                high_hd(m)

            def agg_evac(at, bank):
                act.wait_ge(agg_done, at + 1)
                act.wait_ge(w_done, at + 1)
                a.activation(agg_sb, bank, ACT.Copy,
                             scale=1.0 / (H_SCALE * A_VALUE)).then_inc(agg_out, 1)

            def relu_chunk(m, at):
                act.wait_ge(l_scale, at + 1)
                act.wait_ge(l_split, at + 1)
                for b in range(BC):
                    last = a.activation(hf[:, b, :], x[:, ds(BC * m + b, 1), :]
                                        .rearrange("p a f -> p (a f)"), ACT.Relu,
                                        bias=nb[:, b:b + 1], scale=rs[:, b:b + 1])
                last.then_inc(l_relu, 1)

            def ht_evac(at):
                act.wait_ge(ht_ps, at + 1)
                a.activation(ht_sb, ps_t[:, 0, :], ACT.Copy, scale=1.0 / H_SCALE
                             ).then_inc(ht_out, 1)

            def layer0_chunk(m, bank):
                agg_evac(m, bank)
                relu_chunk(m, m)
                ht_evac(m)

            for m in (0, 1):
                layer0_chunk(m, ps_t[:, m, :])
            with act.Fori(0, NCH // 2 - 1) as i:
                for par in range(2):
                    layer0_chunk(2 * i + 2 + par, ps_acc[:, par, :])
            with act.Fori(0, NCH // 2) as i:
                for par in range(2):
                    agg_evac(NCH + 2 * i + par, ps_acc[:, par, :])
                    relu_chunk(2 * i + par, NCH + 2 * i + par)

            def squares(src, dst, scale=1.0, ready=None, count=0):
                act.drain()
                if ready is not None:
                    act.wait_ge(ready, count)
                for b in range(BC):
                    last = a.activation(act_junk[:, b, :], src(b), ACT.Square, scale=scale,
                                        accum_out=dst(b))
                return last

            def squares_h(m):
                squares(lambda b: hf[:, b, :], lambda b: sq_h[:, ds(BC * m + b, 1)],
                        scale=1.0 / H_SCALE).then_inc(h_sq_in, 1)

            def prep_evac(m, par):
                act.wait_ge(prep_done, NCH + m + 1)
                a.activation(v0[:, BC * par:BC * (par + 1), :], prep_out2[:, :, 0, :], ACT.Copy
                             ).then_inc(v_out, 1)
                squares(lambda b: prep_out2[:, b, 0, :],
                        lambda b: v_sq[:, BC * par + b:BC * par + b + 1]).then_inc(v_sq_in, 1)
                a.activation(hw[:, ds(BC * m, BC), :], prep_out2[:, :, 1, :], ACT.Copy
                             ).then_inc(hw_out, 1)

            def ln_step(k, cut=PAIR):
                act.wait_ge(ln_in, k)
                a.activation(at_l[:, cut], at_u[:, cut], ACT.Ln).then_inc(ln_out, 1)

            def tanh_step(k, src, cut=PAIR):
                act.wait_ge(tanh_in, k)
                a.activation(th[:, cut], src, ACT.Tanh).then_inc(tanh_out, 1)

            def squares_h2(i):
                for par in range(2):
                    squares(lambda b: g_f[:, BC * par + b, :],
                            lambda b: h2_sq[:, BC * par + b:BC * par + b + 1],
                            ready=h2_ok, count=2 * i + par + 1
                            ).then_inc(h2_sq_in, 1)

            agg_evac(2 * NCH, ps_acc[:, 0, :])
            relu_chunk(0, 2 * NCH)
            squares_h(0)
            agg_evac(2 * NCH + 1, ps_acc[:, 1, :])
            ht_evac(NCH)
            relu_chunk(1, 2 * NCH + 1)
            squares_h(1)
            prep_evac(0, 0)
            with act.Fori(0, NCH // 2 - 1) as i:
                m = 2 * i + 2
                ht_evac(NCH + m - 1)
                ln_step(2 * i + 1)
                prep_evac(m - 1, 1)
                tanh_step(i + 1, n_v)
                agg_evac(2 * NCH + m, ps_acc[:, 0, :])
                squares_h2(i)
                ln_step(2 * i + 2)
                agg_evac(2 * NCH + m + 1, ps_acc[:, 1, :])
                relu_chunk(m, 2 * NCH + m)
                squares_h(m)
                ht_evac(NCH + m)
                relu_chunk(m + 1, 2 * NCH + m + 1)
                squares_h(m + 1)
                prep_evac(m, 0)
            i = NCH // 2 - 1
            ht_evac(2 * NCH - 1)
            ln_step(2 * i + 1)
            prep_evac(NCH - 1, 1)
            tanh_step(i + 1, n_v)
            squares_h2(i)
            ln_step(2 * i + 2)

            def layer3_part(i, pars, k):
                banks = (ps_acc[:, 0, :], ps_acc[:, 1, :], ps_t[:, 1, :], ps_t[:, 0, :])
                for par in pars:
                    agg_evac(3 * NCH + 2 * i + par, banks[(2 * i + par) % 4])
                    squares(lambda b: w_out2[:, par, 1, b, :],
                            lambda b: a_sq[:, BC * par + b:BC * par + b + 1],
                            ready=agg_turned, count=2 * i + par + 1
                            ).then_inc(a_sq_in, 1)
                cut = part_cut(pars)
                tanh_step(NCH // 2 + 2 * k + 1, n_a[:, cut], cut)
                for par in pars:
                    squares(lambda b: v0[:, BC * par + b, :],
                            lambda b: v_sq[:, BC * par + b:BC * par + b + 1],
                            ready=v_ok, count=2 * i + par + 1
                            ).then_inc(v_sq_in, 1)
                ln_step(NCH + k + 1, cut)
                tanh_step(NCH // 2 + 2 * k + 2, n_v[:, cut], cut)

            for i in range(NCH // 2 - 1):
                layer3_part(i, (0, 1), i)
            layer3_part(NCH // 2 - 1, (0,), NCH // 2 - 1)
            layer3_part(NCH // 2 - 1, (1,), NCH // 2)

        @block.vector
        def _(dve):
            v = nc.vector
            def scale0(n):
                g = slice(GB * n, GB * (n + 1))
                dve.wait_ge(rstd_ok, n + 1)
                v.tensor_scalar(rs0[:, g], rs0[:, g], H_SCALE, None, ALU.mult)
                dve.drain()
                v.scalar_tensor_tensor(nb0[:, g], mv0[:, g, 0], -1.0, rs0[:, g], ALU.mult,
                                       ALU.mult).then_inc(scale_ok, 1)

            for n in range(NG):
                dve.wait_ge(x_loaded[n], 16)
                for k in range(GB):
                    v.bn_stats(st[:, k, :], x[:, GB * n + k, :])
                dve.drain()
                for k in range(GB):
                    v.bn_aggr(mv0[:, GB * n + k, :], st[:, k, :])
                dve.drain()
                v.tensor_scalar(rs0[:, GB * n:GB * (n + 1)], mv0[:, GB * n:GB * (n + 1), 1],
                                LN_EPS, None, ALU.add).then_inc(stats_ok, 1)
                if n:
                    scale0(n - 1)
            scale0(NG - 1)

            def high_h(n):
                for q in (2 * n, 2 * n + 1):
                    dve.wait_ge(relu_ok, q + 1)
                    dst = h_a[:, BC * q:BC * (q + 1), :, 0:D].rearrange(
                        "p (c t) r f -> p c t r f", t=2)
                    v.tensor_copy(dst[:, :, :, HI, :], h0f[:, 2 * q:2 * q + 2]
                                  ).then_inc(hi_ok, 1)
                    for b in range(BC):
                        k = BC * q + b
                        h = h0f[:, k // 2, k % 2, :]
                        last = v.scalar_tensor_tensor(g_f[:, k % GB, :], h,
                                                      1.0 / (H_SCALE * H_SCALE), h, ALU.mult,
                                                      ALU.mult, accum_out=sq_h[:, k:k + 1])
                last.then_inc(sq_ok, 1)
                dve.drain()

            run_pairs = run0.rearrange("p (c t) -> p c t", t=2)

            def high_u(n):
                g = slice(GB * n, GB * (n + 1))
                dve.wait_ge(norm_ok, n + 1)
                v.tensor_scalar(run0[:, g], norm0[:, g], COS_EPS, None, ALU.max)
                dve.drain()
                v.reciprocal(run0[:, g], run0[:, g])
                dve.drain()
                v.tensor_scalar(run0[:, g], run0[:, g], U_SCALE / H_SCALE, None, ALU.mult)
                dve.drain()
                quarters = [slice(2 * q, 2 * q + 2) for q in (2 * n, 2 * n + 1)]
                for cs in quarters:
                    v.tensor_tensor(u0f[:, cs], h0f[:, cs], run_pairs[:, cs, :].unsqueeze(3)
                                    .broadcast_to([P, 2, 2, D]), ALU.mult)
                dve.drain()
                for cs in quarters:
                    v.tensor_copy(u0p[:, cs, :, HI, :], u0f[:, cs]).then_inc(u_hi_ok, 1)

            def place(m, col, n):
                hh = m // BC
                dve.wait_ge(turned, n + 3)
                v.tensor_copy(adj_t[:, TPH * hh:TPH * (hh + 1), col],
                              ps_t16[:, m % 2, :].bitcast(U16).rearrange("p (c i) -> p c i", i=P)
                              ).then_inc(adj_placed, 1)

            def place_first(m):
                place(m, slice(P * (m % BC), P * (m % BC + 1)), m)

            def x_minus_h(c, blocks):
                v.scalar_tensor_tensor(pairs(x[:, blocks, :]), h0f[:, c, :, :], x_coef,
                                       pairs(x[:, blocks, :]), ALU.mult, ALU.add)
                dve.drain()

            high_h(0)
            for n in range(1, NG):
                high_h(n)
                high_u(n - 1)
                place_first(n - 1)
            high_u(NG - 1)
            place_first(3)

            dve.wait_ge(params_in, 16 * N_PARAMS)
            dve.wait_ge(sig_e, 1)
            v.tensor_scalar(sig_c, e_alpha, 1.0, None, ALU.add)
            v.tensor_scalar(beta_s, beta_c, 1.0 / (U_SCALE * U_SCALE * A_BYTE), None, ALU.mult)
            v.tensor_scalar(shift_c, beta_c, 0.0, -1.0, ALU.max, ALU.mult)
            dve.drain()
            v.reciprocal(sig_c, sig_c)
            v.tensor_scalar(shift_c, shift_c, E_SHIFT, None, ALU.add).then_inc(col_ok, 1)
            dve.drain()
            v.tensor_scalar(sig_h, sig_c, 1.0 / H_SCALE, None, ALU.mult)
            v.tensor_scalar(x_coef, sig_c, 1.0, -1.0 / H_SCALE, ALU.add, ALU.mult)
            for n, (y, y2) in enumerate(((eb_bc, y2_embed), (lb_bc, y2_layer))):
                v.scalar_tensor_tensor(g_f[:, n, :], y, 1.0, y, ALU.mult, ALU.mult, accum_out=y2)
            dve.drain()
            place_first(4)
            place_first(5)
            for q in (NCH - 2, NCH - 1):
                dve.wait_ge(ut_ps, q + 1)
                v.tensor_copy(u_t[:, :, CW * q:CW * (q + 1)],
                              ps_s16[:, q % 4, :].rearrange("p (r i) -> p r i", r=2)
                              ).then_inc(ut_last_ok, 1)
            place_first(6)
            place_first(7)

            def z_step(s, base, col, chunk):
                if s % NB == 0:
                    dve.wait_ge(adj_placed, HPC * (chunk + 1) + 2)
                dve.wait_ge(s_done, base + s + 1)
                k = s % NB
                v.tensor_tensor(ps_s[:, s % RING, :], ps_s[:, s % RING, :],
                                adj_u8[:, k // 2, col, k % 2], ALU.mult).then_inc(z_done, 1)

            def high_part(s, base):
                dve.wait_ge(exp_done, base + s + RING + 1)
                dve.wait_ge(e_used, base + s + 1)
                v.tensor_copy(e_parts[:, HI, s % RING, :], ez[:, s % RING, :]
                              ).then_inc(ehi_done, 1)

            def att_tail(i):
                dve.wait_ge(e_used, NB * (i + 1) + RING)
                v.reciprocal(rec, att_acc[:, :, D])
                dve.drain()
                v.tensor_scalar(rec, rec, sig_h, None, ALU.mult)
                dve.drain()
                for b in range(BC):
                    xb = x[:, ds(BC * i + b, 1), :].rearrange("p a f -> p (a f)")
                    last = v.scalar_tensor_tensor(xb, att_acc[:, b, 0:D], rec[:, b:b + 1], xb,
                                                  ALU.mult, ALU.add)
                    if b % 2:
                        last.then_inc(acc_free, 1)

            def degrees(i):
                cut = ds(BC * i, BC)
                dve.wait_ge(adj_placed, HPC * (i + 1) + 2)
                v.tensor_reduce(deg[:, cut], deg_parts[:, cut, :], mybir.AxisListType.X,
                                ALU.add)
                dve.drain()
                v.tensor_scalar(deg[:, cut], deg[:, cut], 1.0 / A_BYTE, None, ALU.mult)
                dve.drain()
                v.tensor_scalar(dis[:, cut], deg[:, cut], 1.0, None, ALU.max
                                ).then_inc(pow_in, 1)

            def sum_hd(m):
                hm = h_a[:, BC * m:BC * m + BC, :, 0:D]
                v.tensor_tensor(hd_of(m), hm[:, :, HI, :], hm[:, :, LO, :], ALU.add
                                ).then_inc(hd_sum, 1)

            def low_hd(m):
                dve.wait_ge(hd_hi, m + 1)
                dst = h_c[:, BC * m:BC * (m + 1), :, :]
                v.tensor_tensor(dst[:, :, LO, :], hd_of(m), dst[:, :, HI, :], ALU.subtract
                                ).then_inc(hd_ok, 1)

            for s in range(Z_AHEAD):
                z_step(s, 0, slice(0, CW), 0)
            for s in range(EARLY):
                z_step(s + Z_AHEAD, 0, slice(0, CW), 0)
                high_part(s, 0)
            x_minus_h(slice(NP - 2, NP), slice(NB - BC, NB))
            with dve.Fori(0, NCH - 1) as i:
                for s in range(EARLY, NB + EARLY):
                    if s in PLACE_AT:
                        m = PLACE_AT.index(s)
                        place(m, ds(CW * (i + 1) + P * (m % BC), P), HPC * (i + 1) + m)
                    z_s = s + Z_AHEAD
                    z_step(z_s, NB * i, ds(CW * (i + z_s // NB), CW), i + z_s // NB)
                    high_part(s, NB * i)
                    if s == 16:
                        degrees(i)
                    if s == EARLY + 2:
                        x_minus_h(ds(2 * i, 2), ds(BC * i, BC))
                att_tail(i)
            for s in range(EARLY, NB):
                if s + Z_AHEAD < NB:
                    z_step(s + Z_AHEAD, NB * (NCH - 1), slice(CW * (NCH - 1), N), NCH - 1)
                high_part(s, NB * (NCH - 1))
                if s == EARLY:
                    degrees(NCH - 1)
                if s + 1 in HD_AT:
                    sum_hd(HD_AT.index(s + 1))
                if s - 3 in HD_AT:
                    low_hd(HD_AT.index(s - 3))
            rest = range(len(HD_AT), NCH)
            for m in rest[:2]:
                sum_hd(m)
            att_tail(NCH - 1)
            for m in rest:
                low_hd(m)
                if m + 2 < NCH:
                    dve.drain()
                    sum_hd(m + 2)
            v.tensor_scalar(d2, deg, 1.0, None, ALU.add).then_inc(pow_in, 1)
            v.tensor_tensor(inv_deg, deg, l1b, ALU.add)
            dve.drain()
            v.reciprocal(inv_deg, inv_deg)
            dve.drain()
            v.tensor_tensor(inv_beta, inv_deg, l1b, ALU.mult)
            dve.drain()

            def update_x(col, src, m):
                for b in range(BC):
                    xb = x[:, ds(BC * m + b, 1), :].rearrange("p a f -> p (a f)")
                    v.scalar_tensor_tensor(xb, src[:, b, :], col[:, ds(BC * m + b, 1)], xb,
                                           ALU.mult, ALU.add)
                dve.drain()

            def norm_stats(m):
                for b in range(BC):
                    v.bn_stats(st[:, b, :], x[:, ds(BC * m + b, 1), :]
                               .rearrange("p a f -> p (a f)"))
                dve.drain()
                for b in range(BC):
                    v.bn_aggr(mv[:, b, :], st[:, b, :])
                dve.drain()
                v.tensor_scalar(ve, mv[:, :, 1], LN_EPS, None, ALU.add).then_inc(l_stats, 1)

            def norm_scale(L, m):
                dve.wait_ge(l_rstd, NCH * L + m + 1)
                if L == 1:
                    v.scalar_tensor_tensor(rs, ve, H_SCALE, d2[:, ds(BC * m, BC)],
                                           ALU.mult, ALU.mult)
                else:
                    v.tensor_scalar(rs, ve, H_SCALE, None, ALU.mult)
                dve.drain()
                v.scalar_tensor_tensor(nb, mv[:, :, 0], -1.0, rs, ALU.mult, ALU.mult
                                       ).then_inc(l_scale, 1)

            def split(dst, src, done):
                v.tensor_copy(dst[:, :, HI, :], src)
                dve.drain()
                v.tensor_tensor(dst[:, :, LO, :], src, dst[:, :, HI, :], ALU.subtract
                                ).then_inc(done, 1)

            def split_h(L, m):
                dve.wait_ge(l_relu, NCH * L + m + 1)
                split(hs if L == 2 else parts_of(L % 2)[:, ds(BC * m, BC), :, :], hf, l_split)

            dve.wait_ge(pow_ok, NCH + 1)
            with dve.Fori(0, NCH) as m:
                dve.wait_ge(w_done, m + 2)
                update_x(dis, w_out, m)
                norm_stats(m)
                norm_scale(0, m)
                split_h(0, m)
                dve.wait_ge(prep_done, m + 1)
                dve.wait_ge(bias_in, m + 1)
                update_x(inv_beta, prep_out, m)
            with dve.Fori(0, NCH) as m:
                dve.wait_ge(w_done, NCH + m + 2)
                update_x(inv_deg, w_out, m)
                norm_stats(m)
                norm_scale(1, m)
                split_h(1, m)


            def atanh_begin(n, factor, cut=PAIR):
                v.tensor_scalar(at_n[:, cut], n[:, cut], EPS, MAX_TANH, ALU.max, ALU.min)
                v.tensor_scalar(n[:, cut], n[:, cut], EPS, None, ALU.max)
                dve.drain()
                v.tensor_scalar(at_o[:, cut], at_n[:, cut], -1.0, 1.0, ALU.mult, ALU.add)
                dve.drain()
                v.reciprocal(at_o[:, cut], at_o[:, cut])
                dve.drain()
                v.scalar_tensor_tensor(at_t[:, cut], at_n[:, cut], 2.0, at_o[:, cut], ALU.mult,
                                       ALU.mult)
                dve.drain()
                v.tensor_scalar(at_u[:, cut], at_t[:, cut], 1.0, None, ALU.add).then_inc(ln_in, 1)
                dve.drain()
                v.scalar_tensor_tensor(at_w[:, cut], at_u[:, cut], -1.0, n[:, cut], ALU.add,
                                       ALU.mult)
                dve.drain()
                v.reciprocal(at_w[:, cut], at_w[:, cut])
                dve.drain()
                v.scalar_tensor_tensor(at_w[:, cut], at_t[:, cut], 0.5 * factor, at_w[:, cut],
                                       ALU.mult, ALU.mult)
                dve.drain()

            def atanh_end(dst, k, cut=PAIR):
                dve.wait_ge(ln_out, k)
                v.tensor_tensor(dst[:, cut], at_l[:, cut], at_w[:, cut], ALU.mult)
                dve.drain()

            def dot_with(y, ready, count, pars=(0, 1)):
                for par in pars:
                    dve.wait_ge(ready, count + par + 1)
                    for b in range(BC * par, BC * (par + 1)):
                        v.scalar_tensor_tensor(tmp[:, b % BC, :], v0[:, b, :], 1.0, y,
                                               ALU.mult, ALU.mult, accum_out=v_y[:, b:b + 1])
                    dve.drain()

            def exp_map_add(scale, y2, at, k_tanh, pars=(0, 1)):
                cut = part_cut(pars)
                dve.wait_ge(n_v_ok, at + pars[-1] + 1)
                v.tensor_tensor(n_v[:, cut], n_v[:, cut], scale[:, cut], ALU.mult)
                dve.drain()
                v.tensor_scalar(n_v[:, cut], n_v[:, cut], EPS, None, ALU.max).then_inc(tanh_in, 1)
                dve.drain()
                v.reciprocal(th_q[:, cut], n_v[:, cut])
                dve.drain()
                v.tensor_tensor(th_q[:, cut], th_q[:, cut], scale[:, cut], ALU.mult)
                dve.drain()
                v.scalar_tensor_tensor(th_a[:, cut], v_y[:, cut], 2.0, th_q[:, cut], ALU.mult,
                                       ALU.mult)
                v.tensor_tensor(th_x[:, cut], v_sq[:, cut], th_q[:, cut], ALU.mult)
                dve.drain()
                v.tensor_tensor(th_x[:, cut], th_x[:, cut], th_q[:, cut], ALU.mult)
                dve.drain()
                dve.wait_ge(tanh_out, k_tanh)
                v.tensor_tensor(th_q[:, cut], th_q[:, cut], th[:, cut], ALU.mult)
                v.tensor_tensor(th_a[:, cut], th_a[:, cut], th[:, cut], ALU.mult)
                v.tensor_tensor(th_x[:, cut], th_x[:, cut], th[:, cut], ALU.mult)
                dve.drain()
                v.tensor_tensor(x2[:, cut], th_x[:, cut], th[:, cut], ALU.mult)
                v.tensor_scalar(a_c[:, cut], th_a[:, cut], 1.0, None, ALU.add)
                dve.drain()
                v.scalar_tensor_tensor(b_c[:, cut], x2[:, cut], y2, a_c[:, cut], ALU.mult, ALU.add)
                v.scalar_tensor_tensor(th_q[:, cut], a_c[:, cut], y2, th_q[:, cut], ALU.add,
                                       ALU.mult)
                v.tensor_scalar(x2[:, cut], x2[:, cut], -1.0, 1.0, ALU.mult, ALU.add)
                dve.drain()
                v.tensor_scalar(b_c[:, cut], b_c[:, cut], EPS, None, ALU.max)
                dve.drain()
                v.reciprocal(b_c[:, cut], b_c[:, cut])
                dve.drain()
                v.tensor_tensor(a_c[:, cut], th_q[:, cut], b_c[:, cut], ALU.mult)
                v.tensor_tensor(b_c[:, cut], b_c[:, cut], x2[:, cut], ALU.mult)
                dve.drain()

            def layer2_x(m):
                dve.wait_ge(w_done, 2 * NCH + m + 2)
                for b in range(BC):
                    v.scalar_tensor_tensor(tmp[:, b, :], w_out[:, b, :],
                                           d2[:, ds(BC * m + b, 1)], l2_b_bc, ALU.mult, ALU.add)
                dve.drain()
                xc = x[:, ds(BC * m, BC), :]
                v.scalar_tensor_tensor(xc, tmp, 0.0, xc, ALU.max, ALU.add)
                dve.drain()
                norm_stats(m)

            def embed_begin(i):
                dve.wait_ge(n_h_ok, 2 * i + 2)
                atanh_begin(n_h, 1.0)
                atanh_end(l_h, 2 * i + 1)
                dot_with(eb_bc, v_out, 2 * i)
                exp_map_add(l_h, y2_embed, 2 * i, i + 1)
                for b in range(PB):
                    v.tensor_scalar(g_f[:, b, :], eb_bc, b_c[:, b:b + 1], None, ALU.mult)
                dve.drain()
                for b in range(PB):
                    last = v.scalar_tensor_tensor(g_f[:, b, :], v0[:, b, :], a_c[:, b:b + 1],
                                                  g_f[:, b, :], ALU.mult, ALU.add)
                    if b % BC == BC - 1:
                        last.then_inc(h2_ok, 1)

            def log_begin(i):
                dve.wait_ge(n_h2_ok, 2 * i + 2)
                atanh_begin(n_h2, H_SCALE)

            def log_end(i, par):
                cut = slice(BC * par, BC * (par + 1))
                v.tensor_tensor(g_f[:, cut, :], g_f[:, cut, :], l_h[:, cut].unsqueeze(2)
                                .broadcast_to([P, BC, D]), ALU.mult)
                dve.drain()
                split(parts_of(0)[:, ds(BC * (2 * i + par), BC), :, :], g_f[:, cut, :], split_g)

            for m in range(2):
                layer2_x(m)
                norm_scale(2, m)
                split_h(2, m)
            with dve.Fori(0, NCH // 2 - 1) as i:
                m = 2 * i + 2
                embed_begin(i)
                layer2_x(m)
                log_begin(i)
                norm_scale(2, m)
                atanh_end(l_h, 2 * i + 2)
                split_h(2, m)
                layer2_x(m + 1)
                log_end(i, 0)
                norm_scale(2, m + 1)
                log_end(i, 1)
                split_h(2, m + 1)
            embed_begin(NCH // 2 - 1)
            log_begin(NCH // 2 - 1)
            atanh_end(l_h, NCH)
            log_end(NCH // 2 - 1, 0)
            log_end(NCH // 2 - 1, 1)

            def layer3_part(i, pars, k):
                cut = part_cut(pars)
                blocks = range(BC * pars[0], BC * (pars[-1] + 1))
                dve.wait_ge(n_a_ok, 2 * i + pars[-1] + 1)
                v.tensor_scalar(n_a[:, cut], n_a[:, cut], EPS, None, ALU.max
                                ).then_inc(tanh_in, 1)
                dve.drain()
                v.reciprocal(r_a[:, cut], n_a[:, cut])
                dve.drain()
                v.tensor_tensor(cat_sq[:, cut], r_a[:, cut], r_a[:, cut], ALU.mult)
                dve.drain()
                v.tensor_tensor(cat_sq[:, cut], cat_sq[:, cut], a_sq[:, cut], ALU.mult)
                dve.drain()
                dve.wait_ge(tanh_out, NCH // 2 + 2 * k + 1)
                v.tensor_tensor(tq[:, cut], th[:, cut], r_a[:, cut], ALU.mult)
                v.tensor_tensor(cat_sq[:, cut], cat_sq[:, cut], th[:, cut], ALU.mult)
                dve.drain()
                v.tensor_tensor(cat_sq[:, cut], cat_sq[:, cut], th[:, cut], ALU.mult)
                dve.drain()
                v.tensor_tensor(cat_sq[:, cut], cat_sq[:, cut],
                                sq_h[:, ds(PB * i + cut.start, len(blocks))], ALU.add
                                ).then_inc(cat_sq_in, 1)
                dve.wait_ge(w_done, 3 * NCH + 2 * i + pars[-1] + 2)
                for b in blocks:
                    last = v.scalar_tensor_tensor(v0[:, b, :], w_out2[:, b // BC, 0, b % BC, :],
                                                  tq[:, b:b + 1],
                                                  hw[:, ds(PB * i + b, 1), :]
                                                  .rearrange("p a f -> p (a f)"),
                                                  ALU.mult, ALU.add)
                    if b % BC == BC - 1:
                        last.then_inc(v_ok, 1)
                dve.drain()
                dve.wait_ge(n_cat_ok, k + 1)
                atanh_begin(n_cat, 1.0, cut)
                dot_with(lb_bc, v_ok, 2 * i, pars)
                atanh_end(l_h, NCH + k + 1, cut)
                exp_map_add(l_h, y2_layer, NCH + 2 * i, NCH // 2 + 2 * k + 2, pars)
                for par in pars:
                    for b in range(BC * par, BC * (par + 1)):
                        xb = x[:, ds(PB * i + b, 1), :].rearrange("p a f -> p (a f)")
                        v.scalar_tensor_tensor(xb, lb_bc, b_c[:, b:b + 1], xb, ALU.mult, ALU.add)
                    dve.drain()
                    for b in range(BC * par, BC * (par + 1)):
                        xb = x[:, ds(PB * i + b, 1), :].rearrange("p a f -> p (a f)")
                        last = v.scalar_tensor_tensor(xb, v0[:, b, :], a_c[:, b:b + 1], xb,
                                                      ALU.mult, ALU.add)
                    last.then_inc(x_done, 1)

            with dve.Fori(0, NCH // 2 - 1) as i:
                layer3_part(i, (0, 1), i)
            layer3_part(NCH // 2 - 1, (0,), NCH // 2 - 1)
            layer3_part(NCH // 2 - 1, (1,), NCH // 2)

        @block.tensor
        def _(pe):
            t = nc.tensor
            pe.wait_ge(ident_ok, 10)

            def turn(m, half_no):
                pe.wait_ge(cast_done, half_no + 3)
                pe.wait_ge(adj_placed, half_no + 1)
                src = bytes8[:, m % 2, :].bitcast(F16)
                for c in range(TPH):
                    last = t.transpose(ps_t16[:, m % 2, P * c:P * (c + 1)],
                                       src[:, P * c:P * (c + 1)], ident16[:, :])
                last.then_inc(turned, 1)

            def turn_u(q):
                pe.wait_ge(u_ok, q + 1)
                if q >= 4:
                    pe.wait_ge(ut_ok, q - 3)
                dst = ps_s16[:, q % 4, :].rearrange("p (r i) -> p r i", r=2)
                for k in range(BC * q, BC * (q + 1)):
                    for r in (LO, HI):
                        last = t.transpose(dst[:, r, P * (k % BC):P * (k % BC + 1)],
                                           u0p[:, k // 2, k % 2, r, :], ident16[:, :])
                last.then_inc(ut_ps, 1)

            turn(0, 0)
            turn(1, 1)
            turn_u(0)
            turn_u(1)
            turn(2, 2)
            turn_u(2)
            turn_u(3)
            turn(3, 3)
            turn(4, 4)
            turn_u(4)
            turn_u(5)
            turn(5, 5)
            turn(6, 6)
            turn_u(6)
            turn_u(7)
            turn(7, 7)

            def scores(s, base, col):
                pe.wait_ge(exp_done, base + s + 1)
                k = s % NB
                for n, (rj, ri) in enumerate(((HI, HI), (HI, LO), (LO, HI))):
                    last = t.matmul(ps_s[:, s % RING, :], u_t[:, rj, P * k:P * (k + 1)],
                                    u_t[:, ri, col], start=(n == 0), stop=(n == 2))
                last.then_inc(s_done, 1)

            def att_products(s, base, i):
                if s % BC == 0:
                    pe.wait_ge(split0_ok, s // BC + 1)
                pe.wait_ge(elo_done, base + s + RING + 1)
                for b in range(BC):
                    if s == 0 and b % 2 == 0:
                        pe.wait_ge(acc_free, 2 * i + b // 2 + 1)
                    for n, (re, rh) in enumerate(((HI, HI), (HI, LO), (LO, HI))):
                        last = t.matmul(att_acc[:, b, 0:D + 1],
                                        e_parts[:, re, s % RING, P * b:P * (b + 1)],
                                        h_a[:, s, rh, 0:D + 1],
                                        start=(s == 0 and n == 0 and b % 2 == 0),
                                        stop=(s == NB - 1 and n == 2),
                                        skip_group_check=True)
                return last

            for s in range(RING):
                if s < 2:
                    pe.wait_ge(ut_ok, 5 + s)
                else:
                    pe.wait_ge(ut_last_ok, s - 1)
                scores(s, 0, slice(0, CW))
            with pe.Fori(0, NCH - 1) as i:
                for s in range(NB):
                    if s in TURN_AT:
                        m = TURN_AT.index(s)
                        turn(m, HPC * (i + 1) + m)
                    s_s = s + RING
                    scores(s_s, NB * i, ds(CW * (i + s_s // NB), CW))
                    att_products(s, NB * i, i).then_inc(e_used, 1)
            def aggregate(L, c, q):
                h = parts_of((L + 1) % 2)
                if L == 0 and c < 2:
                    acc = ps_t[:, c, :]
                elif L == 3 and c % 4 >= 2:
                    acc = ps_t[:, 3 - c % 4, :]
                else:
                    acc = ps_acc[:, c % 2, :]
                if q == 0:
                    if L == 3 and c >= 2:
                        if c >= 4:
                            pe.wait_ge(agg_out, NCH * L + c - 3)
                        elif c == 3:
                            pe.wait_ge(ht_out, 2 * NCH)
                    elif L == 0 and c < 2:
                        pe.wait_ge(adj_placed, HPC * NCH + 2)
                    elif L == 0 and c < 4:
                        pe.wait_ge(acc_free, 2 * NCH + c - 1)
                    else:
                        pe.wait_ge(agg_out, NCH * L + c - 1)
                if c < (4 if L == 3 else 2):
                    ready, n = ((hd_ok, 0), (l_split, 1), (l_split, NCH + 1), (split_g, 0))[L]
                    pe.wait_ge(ready, n + q + 1)
                if L == 2 and q == NB // BC - 1:
                    for b in range(BC):
                        for r in (LO, HI):
                            t.matmul(acc[:, P * b:P * (b + 1)], h[:, BC * c + b, r, :],
                                     ident16x2[:, :], start=False, stop=False,
                                     skip_group_check=True)
                for k in range(BC * q, BC * (q + 1)):
                    for r in (LO, HI):
                        last = t.matmul(acc, h[:, k, r, :],
                                        adj_f8[:, k // 2, CW * c:CW * (c + 1), k % 2],
                                        start=(k == 0 and r == LO),
                                        stop=(k == NB - 1 and r == HI))
                if q == NB // BC - 1:
                    last.then_inc(agg_done, 1)

            base = NB * (NCH - 1)
            for s in range(NB):
                if s + RING < NB:
                    scores(s + RING, base, slice(CW * (NCH - 1), N))
                att_products(s, base, NCH - 1).then_inc(e_used, 1)
                if s in FILL_AT:
                    aggregate(0, *QUARTERS_0[FILL_AT.index(s)])

            pe.wait_ge(params_in, 16 * N_PARAMS)


            def weights(L, m):
                at = NCH * L + m
                pe.wait_ge(agg_out, at + 1)
                if L < 3:
                    if at:
                        pe.wait_ge(l_stats, at)
                    for b in range(BC):
                        block_t = agg_sb[:, P * b:P * (b + 1)]
                        if L == 0:
                            last = t.transpose(w_out[:, b, :], block_t, ident32)
                        else:
                            last = t.matmul(w_out[:, b, :], block_t,
                                            (kernel_sb, w_sb)[L - 1][:, :], start=True, stop=True)
                else:
                    if m == 0:
                        pe.wait_ge(l_stats, 3 * NCH)
                    elif m == 1:
                        pe.wait_ge(hw_out, NCH)
                    else:
                        pe.wait_ge(v_ok, m - 1)
                    for b in range(BC):
                        last = t.transpose(w_out2[:, m % 2, 1, b, :],
                                           agg_sb[:, P * b:P * (b + 1)], ident32)
                    last.then_inc(agg_turned, 1)
                    for b in range(BC):
                        last = t.matmul(w_out2[:, m % 2, 0, b, :], agg_sb[:, P * b:P * (b + 1)],
                                        layer_bot, start=True, stop=True)
                last.then_inc(w_done, 1)

            def turn_h(L, m):
                pe.wait_ge(l_split, NCH * L + m + 2)
                for b in range(BC):
                    for r in (LO, HI):
                        src = hs[:, b, r, :] if L == 2 else parts_of(0)[:, BC * m + b, r, :]
                        last = t.matmul(ps_t[:, 0, P * b:P * (b + 1)], src, ident16[:, :],
                                        start=(r == LO), stop=(r == HI))
                last.then_inc(ht_ps, 1)

            def prepare(L, m):
                pe.wait_ge(ht_out, NCH * (L // 2) + m + 1)
                for b in range(BC):
                    if L == 0:
                        last = t.matmul(prep_out[:, b, :], ht_sb[:, P * b:P * (b + 1)],
                                        kernel_sb[:, :], start=True, stop=True)
                    else:
                        last = t.matmul(prep_out2[:, b, :, :], ht_sb[:, P * b:P * (b + 1)],
                                        embed_top[:, :, :], start=True, stop=True)
                last.then_inc(prep_done, 1)

            def small_steps(L, idx):
                for steps, after in ((weights, W_AFTER), (turn_h, T_AFTER), (prepare, V_AFTER)):
                    for m, at in enumerate(after[L]):
                        if at == idx:
                            steps(L, m)

            for L in range(4):
                quarters = (QUARTERS_0, QUARTERS, QUARTERS, QUARTERS_3)[L]
                for idx, (c, q) in enumerate(quarters):
                    if L or idx >= len(FILL_AT):
                        aggregate(L, c, q)
                    if L:
                        small_steps(L - 1, idx + len(quarters))
                    small_steps(L, idx)
            weights(3, NCH - 1)


_INS = ["x", "adj", "L0_gnn_alpha", "L0_gnn_beta", "L1_gnn_kernel", "L1_gnn_bias", "L1_gnn_beta",
        "L2_gnn_W", "L2_gnn_b", "L3_gnn_embed", "L3_gnn_layer", "L3_gnn_embed_bias",
        "L3_gnn_layer_bias"]


def kernel(**inputs):
    import numpy as np
    import concourse.bacc as bacc
    from concourse.bass_utils import run_bass_kernel_spmd

    nc = bacc.Bacc("TRN2", target_bir_lowering=False, num_devices=1, dynamic_dma_scratch_size=1024)
    arrays, args = {}, []
    for n in _INS:
        v = np.ascontiguousarray(inputs[n])
        v = v.reshape(v.shape or (1,))
        arrays[f"in_{n}"] = v
        args.append(nc.dram_tensor(f"in_{n}", v.shape, mybir.dt.from_np(v.dtype),
                                   kind="ExternalInput").ap())
    out = nc.dram_tensor("out_0", (N, D), F32, kind="ExternalOutput").ap()
    program(nc, *args, out)
    r = run_bass_kernel_spmd(nc, [arrays], core_ids=[0])
    return r.results[0]["out_0"]
```
